# Optimizing a Trainium2 kernel written in Bass

```python
import numpy as np
import jax
import jax.numpy as jnp

def _softmax(x, axis=-1):
    return jax.nn.softmax(x, axis=axis)

def _gelu(x):
    return jax.nn.gelu(x, approximate=True)

def _silu(x):
    return jax.nn.silu(x)

def _sigmoid(x):
    return jax.nn.sigmoid(x)

def _layernorm(x, axis=-1, eps=1e-05):
    m = jnp.mean(x, axis=axis, keepdims=True)
    v = jnp.var(x, axis=axis, keepdims=True)
    return (x - m) / jnp.sqrt(v + eps)

def _scatter_add(tgt, idx, src, axis=0):
    return tgt.at[idx].add(src)

def _segment_sum(src, seg, n):
    return jax.ops.segment_sum(src, seg, n)
kernel_name = 'mk_xattn_ffn_d1_seqx_r8_6baa46'

def setup_inputs(seed: int=0):
    np.random.seed(seed)
    _w = jnp.asarray

    def _rec_inputs():
        import jax
        import jax.numpy as jnp
        _rk = jax.random.key(seed)
        x = 7.22e-05 + 1 * jax.random.normal(jax.random.fold_in(_rk, 1), (8, 256, 128), jnp.float32)
        _lenS = 256 - jax.random.randint(jax.random.fold_in(_rk, 7), (8,), 0, max(1, 256 // 4) + 1, jnp.int32)
        _lenS2 = 256 - jax.random.randint(jax.random.fold_in(_rk, 8), (8,), 0, max(1, 256 // 4) + 1, jnp.int32)
        _ctx_1024P = jax.random.normal(jax.random.fold_in(_rk, 11), (8, 16, 128), jnp.float32)
        _ctx_1024c = jax.random.dirichlet(jax.random.fold_in(_rk, 511), 0.3 * jnp.ones((16,), jnp.float32), (8, 256))
        _ctx_1024t = jnp.einsum('bsk,bkd->bsd', _ctx_1024c, _ctx_1024P)
        _ctx_1024t = _ctx_1024t * jax.lax.rsqrt(jnp.mean(jnp.square(_ctx_1024t)) + 1e-12) * 0.953939
        ctx_1024 = 4.13588e-05 + 0.999923 * (_ctx_1024t + 0.3 * jax.random.normal(jax.random.fold_in(_rk, 611), (8, 256, 128), jnp.float32))
        return (x, ctx_1024)
    x, ctx_1024 = _rec_inputs()

    def _L0_xattn_setup():
        import jax, jax.numpy as jnp
        import numpy as np
        D_MODEL = 128
        NUM_HEADS = 16
        D_K = D_MODEL // NUM_HEADS

        def _mha(query, key, value, Wq, bq, Wk, bk, Wv, bv, Wo, bo):
            B, S, D = query.shape
            H, dk = (NUM_HEADS, D_K)

            def split_heads(x):
                return x.reshape(B, S, H, dk).transpose(0, 2, 1, 3)
            Q = split_heads(query @ Wq + bq)
            K = split_heads(key @ Wk + bk)
            V = split_heads(value @ Wv + bv)
            scores = jnp.einsum('bhqd,bhkd->bhqk', Q, K) / jnp.sqrt(jnp.float32(dk)).astype(Q.dtype)
            attn = jax.nn.softmax(scores, axis=-1)
            ctx = jnp.einsum('bhqk,bhkd->bhqd', attn, V)
            ctx = ctx.transpose(0, 2, 1, 3).reshape(B, S, D)
            return ctx @ Wo + bo
        key = jax.random.key(seed)
        ks = jax.random.split(key, 11)
        B, S, D = (4, 256, D_MODEL)
        scale = 1.0 / np.sqrt(D)
        inp = {'query': jax.random.normal(ks[0], (B, S, D), jnp.float32), 'key': jax.random.normal(ks[1], (B, S, D), jnp.float32), 'value': jax.random.normal(ks[2], (B, S, D), jnp.float32), 'Wq': jax.random.normal(ks[3], (D, D), jnp.float32) * scale, 'bq': jnp.zeros((D,), jnp.float32), 'Wk': jax.random.normal(ks[4], (D, D), jnp.float32) * scale, 'bk': jnp.zeros((D,), jnp.float32), 'Wv': jax.random.normal(ks[5], (D, D), jnp.float32) * scale, 'bv': jnp.zeros((D,), jnp.float32), 'Wo': jax.random.normal(ks[6], (D, D), jnp.float32) * scale, 'bo': jnp.zeros((D,), jnp.float32)}
        return inp
    _L0_xattn_all = _L0_xattn_setup()
    _L0_xattn_in = {k: v for k, v in _L0_xattn_all.items() if k in ('Wq', 'bq', 'Wk', 'bk', 'Wv', 'bv', 'Wo', 'bo')}
    del _L0_xattn_all

    def _L0_ffn_setup():
        import jax, jax.numpy as jnp
        import numpy as np
        B, S, H, E, K = (2, 128, 128, 8, 2)
        D = 2 * H
        key = jax.random.key(seed)
        ks = jax.random.split(key, 7)
        x = jax.random.normal(ks[0], (B, S, H), dtype=jnp.float32)
        Wr = jax.random.normal(ks[1], (H, E), dtype=jnp.float32) / np.sqrt(H)
        br = jnp.zeros((E,), dtype=jnp.float32)
        W1 = jax.random.normal(ks[2], (E, H, D), dtype=jnp.float32) / np.sqrt(H)
        b1 = jnp.zeros((E, D), dtype=jnp.float32)
        W2 = jax.random.normal(ks[3], (E, D, H), dtype=jnp.float32) / np.sqrt(D)
        b2 = jnp.zeros((E, H), dtype=jnp.float32)
        return {'x': x, 'Wr': Wr, 'br': br, 'W1': W1, 'b1': b1, 'W2': W2, 'b2': b2}
    _L0_ffn_all = _L0_ffn_setup()
    _L0_ffn_in = {k: v for k, v in _L0_ffn_all.items() if k in ('Wr', 'br', 'W1', 'b1', 'W2', 'b2')}
    del _L0_ffn_all
    return {'x': x, 'ctx_1024': ctx_1024, 'L0_xattn_Wq': _L0_xattn_in['Wq'], 'L0_xattn_bq': _L0_xattn_in['bq'], 'L0_xattn_Wk': _L0_xattn_in['Wk'], 'L0_xattn_bk': _L0_xattn_in['bk'], 'L0_xattn_Wv': _L0_xattn_in['Wv'], 'L0_xattn_bv': _L0_xattn_in['bv'], 'L0_xattn_Wo': _L0_xattn_in['Wo'], 'L0_xattn_bo': _L0_xattn_in['bo'], 'L0_ffn_Wr': _L0_ffn_in['Wr'], 'L0_ffn_br': _L0_ffn_in['br'], 'L0_ffn_W1': _L0_ffn_in['W1'], 'L0_ffn_b1': _L0_ffn_in['b1'], 'L0_ffn_W2': _L0_ffn_in['W2'], 'L0_ffn_b2': _L0_ffn_in['b2']}

def reference(x, ctx_1024, L0_xattn_Wq, L0_xattn_bq, L0_xattn_Wk, L0_xattn_bk, L0_xattn_Wv, L0_xattn_bv, L0_xattn_Wo, L0_xattn_bo, L0_ffn_Wr, L0_ffn_br, L0_ffn_W1, L0_ffn_b1, L0_ffn_W2, L0_ffn_b2):
    import jax
    import jax.numpy as jnp

    def _L0_xattn_ref(query, key, value, Wq, bq, Wk, bk, Wv, bv, Wo, bo):
        import jax, jax.numpy as jnp
        import numpy as np
        D_MODEL = 128
        NUM_HEADS = 16
        D_K = D_MODEL // NUM_HEADS

        def _mha(query, key, value, Wq, bq, Wk, bk, Wv, bv, Wo, bo):
            B, S, D = query.shape
            H, dk = (NUM_HEADS, D_K)

            def split_heads(x):
                return x.reshape(B, S, H, dk).transpose(0, 2, 1, 3)
            Q = split_heads(query @ Wq + bq)
            K = split_heads(key @ Wk + bk)
            V = split_heads(value @ Wv + bv)
            scores = jnp.einsum('bhqd,bhkd->bhqk', Q, K) / jnp.sqrt(jnp.float32(dk)).astype(Q.dtype)
            attn = jax.nn.softmax(scores, axis=-1)
            ctx = jnp.einsum('bhqk,bhkd->bhqd', attn, V)
            ctx = ctx.transpose(0, 2, 1, 3).reshape(B, S, D)
            return ctx @ Wo + bo
        return _mha(query, key, value, Wq, bq, Wk, bk, Wv, bv, Wo, bo)

    def _L0_ffn_ref(x, Wr, br, W1, b1, W2, b2):
        import jax, jax.numpy as jnp
        import numpy as np
        B, S, H, E, K = (2, 128, 128, 8, 2)
        D = 2 * H
        logits = jnp.einsum('bsh,he->bse', x, Wr) + br
        probs = jax.nn.softmax(logits, axis=-1)
        top_p, top_i = jax.lax.top_k(probs, K)
        cw = jnp.sum(jax.nn.one_hot(top_i, E, dtype=x.dtype) * top_p[..., None], axis=-2)
        h = jax.nn.relu(jnp.einsum('bsh,ehd->bsed', x, W1) + b1)
        y = jnp.einsum('bsed,edh->bseh', h, W2) + b2
        out = jnp.einsum('bseh,bse->bsh', y, cw)
        return out
    x = x + _L0_xattn_ref(_layernorm(x, axis=-1), ctx_1024, ctx_1024, L0_xattn_Wq, L0_xattn_bq, L0_xattn_Wk, L0_xattn_bk, L0_xattn_Wv, L0_xattn_bv, L0_xattn_Wo, L0_xattn_bo)
    x = x + _L0_ffn_ref(_layernorm(x, axis=-1), L0_ffn_Wr, L0_ffn_br, L0_ffn_W1, L0_ffn_b1, L0_ffn_W2, L0_ffn_b2)
    return x

_drawn_inputs = setup_inputs


def setup_inputs(seed=0):
    import zlib

    import numpy as np

    out = dict(_drawn_inputs(seed))
    spreads = {'L0_xattn_bq': (0.0, 0.1),
     'L0_xattn_bk': (0.0, 0.8),
     'L0_xattn_bv': (0.0, 0.1),
     'L0_xattn_bo': (0.0, 0.1),
     'L0_ffn_br': (0.0, 0.1),
     'L0_ffn_b1': (0.0, 0.308),
     'L0_ffn_b2': (0.0, 0.1)}
    factors = {}
    for name, (base, spread) in spreads.items():
        noise = np.random.default_rng([zlib.crc32(name.encode()), seed]).standard_normal(out[name].shape)
        drawn = base * np.exp(spread * noise) if base else spread * noise
        out[name] = jnp.asarray(drawn.astype(out[name].dtype))
    for name, factor in factors.items():
        out[name] = (out[name] * factor).astype(out[name].dtype)
    return out
```

```python
import concourse.bass as bass
from concourse import mybir
from contextlib import ExitStack

F32 = mybir.dt.float32
F32R = mybir.dt.float32r
U32 = mybir.dt.uint32
ALU = mybir.AluOpType
ACT = mybir.ActivationFunctionType
AX = mybir.AxisListType

B, S, D = 8, 256, 128
H, DK = 16, 8
E, DF = 8, 256
P = 128
NT = S // P
TILES = E * DF // P
HG = 8
SHIFT_ROW = 4 * DK
EPS = 1e-5
EXP_SCALE = float(DK) ** -0.5
P_BUFS = 8
G_BUFS = 4
W2_LAG = 2
SLOTS = 16

LAG_A, LAG_M, LAG_B, LAG_C, LAG_D = 0, 1, 2, 3, 4
STEPS = B + LAG_D
MISC = {"shift1": 0, "heads": 1, "ctxT": 2, "wo": 3, "inT": 4, "qk": 5, "x2T": 6, "router": 7,
        "v": 8, "shift0": 9, "cwT": 10}
MISC_LAG = {"shift1": LAG_B, "heads": LAG_C, "ctxT": LAG_C, "wo": LAG_C, "inT": LAG_A, "qk": LAG_A,
            "x2T": LAG_C, "router": LAG_C, "v": LAG_M, "shift0": LAG_M, "cwT": LAG_C}
SETUP_STEP = 1
LOADS_QKV, LOADS_W2, LOADS_TAIL = 5 + NT, 3, 2 + 2 * NT
STACK_DMAS, SHIFT_DMAS = 9, 2
ROUTE_CHAIN = 8


class Batch:

    def __init__(self, t, c):
        self.t, self.c = t, c
        self.n = 2 * t + c
        self.par = c % 2

    def back(self, lag):
        return Batch(self.t, self.c - lag)

    def live(self):
        return not isinstance(self.n, int) or 0 <= self.n < B


def head_of(n):
    g, j, c = n // HG, n // 4 % 2, n % 4
    return g * HG + c * 2 + j


def wait_alone(eng, semaphore, value):
    if not isinstance(value, int):
        value = eng.to_reg(value)
        eng.wait_ge(semaphore, 1)
    eng.wait_ge(semaphore, value)


def steps(eng, one_step):
    first, last = LAG_D, B
    for c in range(first):
        one_step(Batch(0, c))
    with eng.Fori(first // 2, last // 2) as t:
        one_step(Batch(t, 0))
        one_step(Batch(t, 1))
    for c in range(last, STEPS):
        one_step(Batch(0, c))


def xattn_moe(nc, x, ctx_in, Wq, bq, Wk, bk, Wv, bv, Wo, bo, Wr, br, W1, b1, W2, b2, out):
    es = ExitStack()
    with es:
        def sb(name, shape, dt=F32):
            return es.enter_context(nc.sbuf_tensor(name, shape, dt))

        def ps(name, shape):
            return es.enter_context(nc.psum_tensor(name, shape, F32))

        def sem(name):
            return es.enter_context(nc.semaphore(name))

        x_all = sb("x_all", [P, B * NT, D])
        c_all = sb("c_all", [P, B * NT, D])
        c_cur = sb("c_cur", [P, 2, NT, D])
        xn = sb("xn", [P, 2, NT, D])
        inT = sb("inT", [P, 2, 2, S])
        q_hi = sb("q_hi", [P, 2, S], F32R)
        q_lo = sb("q_lo", [P, 2, S], F32R)
        k_hi = sb("k_hi", [P, 2, S], F32R)
        k_lo = sb("k_lo", [P, 2, S], F32R)
        Qs = [sb(f"Qs{n}", [P, H, S], F32R) for n in range(2)]
        Ks = [sb(f"Ks{n}", [P, H, S], F32R) for n in range(2)]
        v_pad = sb("v_pad", [P, 2, NT, H, 32])
        negm = sb("negm", [P, 2, NT, H])
        sh_hi = sb("sh_hi", [HG, 2, S], F32R)
        sh_lo = sb("sh_lo", [HG, 2, S], F32R)
        zero_rows = sb("zero_rows", [2, HG * S])
        probs = sb("probs", [P, P_BUFS, NT, S])
        oT = sb("oT", [P, 2, S])
        rden = sb("rden", [P, NT, H])
        ctxn = sb("ctxn", [P, NT, H, DK])
        ctxT = sb("ctxT", [P, S])
        stats = sb("stats", [P, 2, NT, 6])
        mv = sb("mv", [P, 2, NT, 2])
        rstd = sb("rstd", [P, 2, NT])
        var_eps = sb("var_eps", [P, 2, NT])
        x2n = sb("x2n", [P, NT, D])
        x2T = sb("x2T", [P, S])
        x2T_hi = sb("x2T_hi", [P, 2, S], F32R)
        x2T_lo = sb("x2T_lo", [P, 2, S], F32R)
        logits = sb("logits", [P, NT, E])
        top = sb("top", [P, NT, 8])
        top_i = sb("top_i", [P, NT, 8], U32)
        top_f = sb("top_f", [P, NT, 8])
        shifted = sb("shifted", [P, NT, E])
        pexp = sb("pexp", [P, NT, E])
        psum_e = sb("psum_e", [P, NT])
        rsum_e = sb("rsum_e", [P, NT])
        pick1 = sb("pick1", [P, NT, E])
        pick2 = sb("pick2", [P, NT, E])
        picked = sb("picked", [P, NT, E])
        cw = sb("cw", [P, NT, E])
        cwT = sb("cwT", [E, 2, S])
        cw_b = sb("cw_b", [P, 2, E, S])
        g_t = sb("g_t", [P, G_BUFS, S])
        yT = sb("yT", [P, S])
        ident = sb("ident", [P, P])
        empty_turn = sb("empty_turn", [P, 1])
        eps = sb("eps", [P, NT])
        half = sb("half", [P, NT])
        expert_no = sb("expert_no", [P, E])
        wq = sb("wq", [P, D])
        wk = sb("wk", [P, D])
        wv = sb("wv", [P, D])
        wo = sb("wo", [P, D])
        wr = sb("wr", [P, E])
        bq_c = sb("bq_c", [P, 1])
        bk_c = sb("bk_c", [P, 1])
        bv_b = sb("bv_b", [P, NT, D])
        bo_b = sb("bo_b", [P, NT, D])
        br_b = sb("br_b", [P, NT, E])
        w1_in = sb("w1_in", [P, TILES, P])
        w1_hi = sb("w1_hi", [P, TILES, P], F32R)
        w1_lo = sb("w1_lo", [P, TILES, P], F32R)
        w2 = sb("w2", [P, TILES, P])
        b1_in = sb("b1_in", [P, TILES])
        b1_neg = sb("b1_neg", [P, TILES])
        b1_cols = sb("b1_cols", [P, TILES, E])
        b2_in = sb("b2_in", [E, D])
        bias2 = sb("bias2", [E, D])

        s_bank = [ps(f"s_bank{n}", [P, NT, S]) for n in range(2)]
        m_bank = ps("m_bank", [P, NT, S])
        o_bank = ps("o_bank", [P, 2, S])
        z_bank = [ps(f"z_bank{n}", [P, 512]) for n in range(2)]
        y_bank = ps("y_bank", [P, 512])
        misc = ps("misc", [P, 512])

        cw_dram = nc.dram_tensor("cw_scratch", (2, E, S), F32, kind="Internal").ap()

        x0_loaded = sem("x0_loaded")
        x_loaded = sem("x_loaded")
        c0_loaded = sem("c0_loaded")
        c_loaded = sem("c_loaded")
        wqkv_loaded = sem("wqkv_loaded")
        wtail_loaded = sem("wtail_loaded")
        w1_loaded = sem("w1_loaded")
        w2_loaded = sem("w2_loaded")
        const_ready = sem("const_ready")
        ident_step = sem("ident_step")
        w1_hi_ready = sem("w1_hi_ready")
        w1_ready = sem("w1_ready")
        q_rows_ready = sem("q_rows_ready")
        k_zero = sem("k_zero")
        k_rows_ready = sem("k_rows_ready")
        v_zero = sem("v_zero")
        v_cols_ready = sem("v_cols_ready")
        b1_neg_ready = sem("b1_neg_ready")
        b1_cols_ready = sem("b1_cols_ready")
        bias2_ready = sem("bias2_ready")
        setup_bias2 = sem("setup_bias2")
        stat_ready = [sem("ln1_stat_ready"), sem("ln2_stat_ready")]
        aggr_ready = [sem("ln1_aggr_ready"), sem("ln2_aggr_ready")]
        vareps_ready = [sem("ln1_vareps_ready"), sem("ln2_vareps_ready")]
        rstd_ready = [sem("ln1_rstd_ready"), sem("ln2_rstd_ready")]
        xn_ready = sem("xn_ready")
        c_cur_ready = sem("c_cur_ready")
        xbo_ready = sem("xbo_ready")
        inT_ps = sem("inT_ps")
        inT_ready = sem("inT_ready")
        qk_ps = sem("qk_ps")
        qk_hi_ready = sem("qk_hi_ready")
        qk_lo_ready = sem("qk_lo_ready")
        v_ps = sem("v_ps")
        v_ready = sem("v_ready")
        stacked = [sem("stacked0"), sem("stacked1")]
        m_ready = sem("m_ready")
        negm_ready = sem("negm_ready")
        shift_ps = [sem("shift0_ps"), sem("shift1_ps")]
        shift_hi = [sem("shift0_hi"), sem("shift1_hi")]
        shift_lo = [sem("shift0_lo"), sem("shift1_lo")]
        shifts_in = [sem("shift0_in"), sem("shift1_in")]
        s_ready = sem("s_ready")
        p_ready = sem("p_ready")
        p_used = sem("p_used")
        o_taken = sem("o_taken")
        heads_ps = sem("heads_ps")
        rden_ready = sem("rden_ready")
        ctxn_ready = sem("ctxn_ready")
        ctxT_ps = sem("ctxT_ps")
        ctxT_ready = sem("ctxT_ready")
        wo_ps = sem("wo_ps")
        x2_ready = sem("x2_ready")
        x2n_ready = sem("x2n_ready")
        x2T_ps = sem("x2T_ps")
        x2T_copy = sem("x2T_copy")
        x2T_ready = sem("x2T_ready")
        router_ps = sem("router_ps")
        logits_ready = sem("logits_ready")
        route_step = sem("route_step")
        shifted_ready = sem("shifted_ready")
        pexp_ready = sem("pexp_ready")
        cw_ready = sem("cw_ready")
        cwT_ps = sem("cwT_ps")
        cwT_ready = sem("cwT_ready")
        cw_stored = sem("cw_stored")
        cw_b_ready = sem("cw_b_ready")
        z_ready = sem("z_ready")
        g_ready = sem("g_ready")
        y_ready = sem("y_ready")
        y_taken = sem("y_taken")
        out_ps = sem("out_ps")
        out_ready = sem("out_ready")
        stored = sem("stored")

        block = es.enter_context(nc.Block())

        @block.sync
        def _(sp):
            sp.dma_start(x_all[:, 0:NT, :], x[:, 0:NT, :]).then_inc(x0_loaded, 16)
            sp.dma_start(c_all[:, 0:NT, :], ctx_in[:, 0:NT, :]).then_inc(c0_loaded, 16)
            sp.dma_start(wq[:, :], Wq).then_inc(wqkv_loaded, 16)
            sp.dma_start(wk[:, :], Wk).then_inc(wqkv_loaded, 16)
            sp.dma_start(wv[:, :], Wv).then_inc(wqkv_loaded, 16)
            sp.dma_start(bq_c[:, :], bq).then_inc(wqkv_loaded, 16)
            sp.dma_start(bk_c[:, :], bk).then_inc(wqkv_loaded, 16)
            for t in range(NT):
                sp.dma_start(bv_b[:, t, :], bv.broadcast_to([P, D])).then_inc(wqkv_loaded, 16)
            sp.dma_start(x_all[:, NT:, :], x[:, NT:, :]).then_inc(x_loaded, 16)
            sp.dma_start(c_all[:, NT:, :], ctx_in[:, NT:, :]).then_inc(c_loaded, 16)
            for t in range(NT):
                sp.dma_start(bo_b[:, t, :], bo.broadcast_to([P, D])).then_inc(wtail_loaded, 16)
                sp.dma_start(br_b[:, t, :], br.broadcast_to([P, E])).then_inc(wtail_loaded, 16)
            sp.dma_start(wo[:, :], Wo).then_inc(wtail_loaded, 16)
            sp.dma_start(wr[:, :], Wr).then_inc(wtail_loaded, 16)
            sp.dma_start(w1_in[:, :, :], W1).then_inc(w1_loaded, 16)
            sp.dma_start(w2[:, :, :], W2).then_inc(w2_loaded, 16)
            sp.dma_start(b1_in[:, :], b1).then_inc(w2_loaded, 16)
            sp.dma_start(b2_in[:, :], b2).then_inc(w2_loaded, 16)

            def stack(b, g):
                heads = slice(HG * g, HG * (g + 1))
                rows = slice(64 * g, 64 * g + 64)
                sp.wait_ge(qk_lo_ready, 2 * b.n + 2)
                if isinstance(b.n, int) and b.n < 2:
                    sp.wait_ge(q_rows_ready, b.n + 1)
                    sp.wait_ge(k_rows_ready, b.n + 1)
                for r, (q, k) in enumerate(((q_hi, k_hi), (q_hi, k_lo), (q_lo, k_hi), (q_lo, k_lo))):
                    part = slice(DK * r, DK * (r + 1))
                    sp.dma_start(Qs[b.par][part, heads, :].bitcast(F32), q[rows, b.par, :].bitcast(F32))\
                      .then_inc(stacked[g], 16)
                    sp.dma_start(Ks[b.par][part, heads, :].bitcast(F32), k[rows, b.par, :].bitcast(F32))\
                      .then_inc(stacked[g], 16)
                sp.dma_start(Qs[b.par][SHIFT_ROW:SHIFT_ROW + 2, heads, :].bitcast(F32), zero_rows[:, :])\
                  .then_inc(stacked[g], 16)

            def shift(b, g):
                heads = slice(HG * g, HG * (g + 1))
                sp.wait_ge(shift_lo[g], b.n + 1)
                for r, part in enumerate((sh_hi, sh_lo)):
                    row = slice(SHIFT_ROW + r, SHIFT_ROW + r + 1)
                    sp.dma_start(Qs[b.par][row, heads, :].bitcast(F32), part[:, g, :].bitcast(F32))\
                      .then_inc(shifts_in[g], 16)

            def one_step(i):
                a, m, bb, cc, dd = (i.back(lag) for lag in (LAG_A, LAG_M, LAG_B, LAG_C, LAG_D))
                if bb.live():
                    shift(bb, 1)
                if a.live():
                    if bb.live():
                        sp.wait_ge(s_ready, H * bb.n + HG)
                    stack(a, 0)
                if m.live():
                    shift(m, 0)
                if cc.live():
                    sp.wait_ge(cwT_ready, cc.n + 1)
                    if not isinstance(cc.n, int) or cc.n >= 1:
                        sp.wait_ge(cw_b_ready, 16 * cc.n)
                    sp.dma_start(cw_dram[cc.par], cwT[:, cc.par, :]).then_inc(cw_stored, 16)
                    sp.wait_ge(cw_stored, 16 * cc.n + 16)
                    sp.dma_start(cw_b[:, cc.par, :, :],
                                 cw_dram[cc.par:cc.par + 1].broadcast_to([P, E, S])).then_inc(cw_b_ready, 16)
                if a.live():
                    if bb.live():
                        sp.wait_ge(s_ready, H * bb.n + H)
                    stack(a, 1)
                if dd.live():
                    wait_alone(sp, out_ready, dd.n + 2)
                    sp.dma_start(out[:, bass.ds(NT * dd.n, NT), :],
                                 x_all[:, bass.ds(NT * dd.n, NT), :]).then_inc(stored, 16)

            steps(sp, one_step)
            sp.wait_ge(stored, 16 * B)

        @block.gpsimd
        def _(pool):
            pool.memset(ident[:, :], 0.0).then_inc(ident_step, 1)
            pool.wait_ge(ident_step, 1)
            pool.affine_select(out=ident[:, :], in_=ident[:, :], compare_op=ALU.not_equal, fill=1.0,
                               base=0, pattern=[[-1, P]], channel_multiplier=1).then_inc(ident_step, 1)
            pool.memset(Qs[0][:, :, :].bitcast(F32), 0.0).then_inc(q_rows_ready, 1)
            pool.memset(half[:, :], -0.5)
            pool.memset(eps[:, :], EPS)
            pool.memset(zero_rows[:, :], 0.0)
            for e in range(E):
                pool.memset(expert_no[:, e:e + 1], float(e))
            pool.memset(b1_cols[:, :, :], 0.0).then_inc(const_ready, 1)

            def inverse_root(b, ln):
                pool.wait_ge(aggr_ready[ln], NT * b.n + NT)
                pool.tensor_tensor(var_eps[:, ln, :], mv[:, ln, :, 1], eps[:, :], ALU.add)\
                    .then_inc(vareps_ready[ln], 1)
                pool.wait_ge(vareps_ready[ln], b.n + 1)
                pool.tensor_tensor(rstd[:, ln, :], var_eps[:, ln, :], half[:, :], ALU.pow)\
                    .then_inc(rstd_ready[ln], 1)

            def one_step(i):
                a, cc = i.back(LAG_A), i.back(LAG_C)
                if a.live():
                    if isinstance(a.n, int) and a.n == 0:
                        pool.wait_ge(c0_loaded, 16)
                    else:
                        pool.wait_ge(c_loaded, 16)
                    if not isinstance(a.n, int) or a.n >= 2:
                        pool.wait_ge(inT_ps, a.n - 1)
                    pool.tensor_copy(c_cur[:, a.par, :, :], c_all[:, bass.ds(NT * a.n, NT), :])\
                        .then_inc(c_cur_ready, 1)
                    inverse_root(a, 0)
                    pool.wait_ge(wtail_loaded, 16 * LOADS_TAIL)
                    pool.wait_ge(xn_ready, NT * a.n + NT)
                    xb = x_all[:, bass.ds(NT * a.n, NT), :]
                    pool.tensor_tensor(xb, xb, bo_b[:, :, :], ALU.add).then_inc(xbo_ready, 1)
                if isinstance(i.n, int) and i.n == 0:
                    pool.memset(Qs[1][:, :, :].bitcast(F32), 0.0).then_inc(q_rows_ready, 1)
                if isinstance(i.n, int) and i.n == SETUP_STEP:
                    pool.wait_ge(w2_loaded, 16 * LOADS_W2)
                    for e in range(E):
                        last = pool.tensor_copy(b1_cols[:, 2 * e:2 * e + 2, e], b1_in[:, 2 * e:2 * e + 2])
                    last.then_inc(b1_cols_ready, 1)
                if cc.live():
                    inverse_root(cc, 1)

            pool.wait_ge(const_ready, 1)
            steps(pool, one_step)

        @block.scalar
        def _(act):
            def split_hi(b, g):
                act.wait_ge(shift_ps[g], b.n + 1)
                act.activation(sh_hi[:, g, :], misc[0:HG, 0:S], ACT.Copy).then_inc(shift_hi[g], 1)

            def one_step(i):
                a, m, bb, cc, dd = (i.back(lag) for lag in (LAG_A, LAG_M, LAG_B, LAG_C, LAG_D))
                if isinstance(i.n, int) and i.n == SETUP_STEP:
                    act.wait_ge(w1_loaded, 16)
                    act.activation(w1_hi[:, :, :], w1_in[:, :, :], ACT.Copy).then_inc(w1_hi_ready, 1)
                for s in range(SLOTS):
                    if bb.live():
                        n = H * bb.n + s
                        act.wait_ge(s_ready, n + 1)
                        if s % 4 == 0 and (not isinstance(bb.n, int) or bb.n > 0 or s >= P_BUFS):
                            act.wait_ge(p_used, 4 * bb.n + s // 4 + 1 - P_BUFS // 4)
                        act.activation(probs[:, s % P_BUFS, :, :], s_bank[s % 2][:, :, :], ACT.Exp,
                                       scale=EXP_SCALE).then_inc(p_ready, 1)
                    if s == MISC["shift1"] and bb.live():
                        split_hi(bb, 1)
                    if s == MISC["ctxT"] and cc.live():
                        act.wait_ge(ctxT_ps, cc.n + 1)
                        act.activation(ctxT[:, :], misc[:, 0:S], ACT.Copy).then_inc(ctxT_ready, 1)
                    if s == MISC["inT"] and a.live():
                        act.wait_ge(inT_ps, a.n + 1)
                        act.activation(inT[:, a.par, :, :], misc[:, :].rearrange("p (w t) -> p w t", w=2),
                                       ACT.Copy).then_inc(inT_ready, 1)
                    if s == MISC["qk"] and a.live():
                        act.wait_ge(qk_ps, a.n + 1)
                        act.activation(q_hi[:, a.par, :], misc[:, 0:S], ACT.Identity, bias=bq_c[:, :])\
                           .then_inc(qk_hi_ready, 1)
                        act.activation(k_hi[:, a.par, :], misc[:, S:2 * S], ACT.Identity, bias=bk_c[:, :])\
                           .then_inc(qk_hi_ready, 1)
                    if s == MISC["x2T"] and cc.live():
                        act.wait_ge(x2T_ps, cc.n + 1)
                        act.activation(x2T[:, :], misc[:, 0:S], ACT.Copy).then_inc(x2T_copy, 1)
                        act.activation(x2T_hi[:, cc.par, :], misc[:, 0:S], ACT.Copy).then_inc(x2T_copy, 1)
                    if s == MISC["router"] + 1 and cc.live():
                        act.wait_ge(shifted_ready, cc.n + 1)
                        act.activation(pexp[:, :, :], shifted[:, :, :], ACT.Exp).then_inc(pexp_ready, 1)
                    if s == MISC["shift0"] and m.live():
                        split_hi(m, 0)
                    if s == MISC["cwT"] and cc.live():
                        act.wait_ge(cwT_ps, cc.n + 1)
                        act.activation(cwT[:, cc.par, :], misc[0:E, 0:S], ACT.Copy).then_inc(cwT_ready, 1)
                if dd.live():
                    act.wait_ge(y_ready, dd.n + 1)
                    act.activation(yT[:, :], y_bank[:, 0:S], ACT.Copy).then_inc(y_taken, 1)
                if bb.live():
                    act.wait_ge(p_used, 4 * bb.n + 4)
                    act.activation(oT[:, :, :], o_bank[:, :, :], ACT.Copy).then_inc(o_taken, 1)

            steps(act, one_step)

        @block.vector
        def _(dve):
            def key_rows(n):
                dve.memset(Ks[n][:, :, :].bitcast(F32), 0.0).then_inc(k_zero, 1)
                dve.wait_ge(k_zero, n + 1)
                dve.memset(Ks[n][SHIFT_ROW:SHIFT_ROW + 2, :, :].bitcast(F32), 1.0).then_inc(k_rows_ready, 1)

            key_rows(0)
            dve.memset(empty_turn[:, :], 0.0).then_inc(out_ready, 1)

            def statistics(b, ln, src):
                for t in range(NT):
                    last = dve.bn_stats(stats[:, ln, t, :], src(t))
                last.then_inc(stat_ready[ln], 1)
                wait_alone(dve, stat_ready[ln], b.n + 1)
                for t in range(NT):
                    dve.bn_aggr(mv[:, ln, t, :], stats[:, ln, t, :]).then_inc(aggr_ready[ln], 1)

            def normalise(b, ln, src, dst, done):
                dve.wait_ge(rstd_ready[ln], b.n + 1)
                for t in range(NT):
                    dve.tensor_scalar(dst(t), src(t), mv[:, ln, t, 0:1], rstd[:, ln, t:t + 1],
                                      ALU.subtract, ALU.mult).then_inc(done, 1)

            def split_lo(b, g):
                dve.wait_ge(shift_hi[g], b.n + 1)
                dve.tensor_tensor(sh_lo[:, g, :], misc[0:HG, 0:S], sh_hi[:, g, :].bitcast(F32), ALU.subtract)\
                   .then_inc(shift_lo[g], 1)

            def x_tile(b):
                return lambda t: x_all[:, bass.ds(NT * b.n + t, 1), :]

            def x_batch(b):
                return x_all[:, bass.ds(NT * b.n, NT), :]

            def route(b):
                links = [0]

                def link(ins):
                    links[0] += 1
                    ins.then_inc(route_step, 1)
                    dve.wait_ge(route_step, ROUTE_CHAIN * b.n + links[0])

                dve.wait_ge(router_ps, b.n + 1)
                dve.tensor_tensor(logits[:, :, :], misc[:, 0:NT * E].rearrange("p (t e) -> p t e", t=NT),
                                  br_b[:, :, :], ALU.add).then_inc(logits_ready, 1)
                wait_alone(dve, logits_ready, b.n + 1)
                dve.max(out=top[:, 0, :], in_=logits[:, 0, :])
                link(dve.max(out=top[:, 1, :], in_=logits[:, 1, :]))
                dve.tensor_tensor(shifted[:, :, :], logits[:, :, :], top[:, :, 0:1].broadcast_to([P, NT, E]),
                                  ALU.subtract).then_inc(shifted_ready, 1)
                dve.max_index(top_i[:, 0, :], top[:, 0, :], logits[:, 0, :])
                link(dve.max_index(top_i[:, 1, :], top[:, 1, :], logits[:, 1, :]))
                link(dve.tensor_copy(top_f[:, :, :], top_i[:, :, :]))
                dve.wait_ge(pexp_ready, b.n + 1)
                link(dve.tensor_reduce(psum_e[:, :], pexp[:, :, :], AX.X, ALU.add))
                link(dve.reciprocal(rsum_e[:, :], psum_e[:, :]))
                for t in range(NT):
                    for pick, k in ((pick1, 0), (pick2, 1)):
                        ins = dve.scalar_tensor_tensor(pick[:, t, :], expert_no[:, :], top_f[:, t, k:k + 1],
                                                       pexp[:, t, :], op0=ALU.is_equal, op1=ALU.mult)
                        if k == 1:
                            link(ins)
                link(dve.tensor_tensor(picked[:, :, :], pick1[:, :, :], pick2[:, :, :], ALU.add))
                dve.tensor_tensor(cw[:, :, :], picked[:, :, :],
                                  rsum_e[:, :].rearrange("p (t o) -> p t o", o=1).broadcast_to([P, NT, E]),
                                  ALU.mult).then_inc(cw_ready, 1)
                assert links[0] == ROUTE_CHAIN

            def one_step(i):
                a, m, bb, cc, dd = (i.back(lag) for lag in (LAG_A, LAG_M, LAG_B, LAG_C, LAG_D))
                static = isinstance(i.n, int)
                for s in range(SLOTS):
                    if m.live():
                        dve.wait_ge(m_ready, H * m.n + s + 1)
                        dve.tensor_reduce(negm[:, m.par, :, s], m_bank[:, :, :], AX.X, ALU.max, negate=True)\
                           .then_inc(negm_ready, 1)
                    if dd.live():
                        dve.wait_ge(z_ready, TILES * dd.n + s + 1)
                        if s == 0:
                            dve.wait_ge(cw_b_ready, 16 * dd.n + 16)
                        dve.scalar_tensor_tensor(g_t[:, s % G_BUFS, :], z_bank[s % 2][:, 0:S], b1_neg[:, s:s + 1],
                                                 cw_b[:, dd.par, s // 2, :], op0=ALU.max, op1=ALU.mult)\
                           .then_inc(g_ready, 1)
                    if s == 0 and a.live():
                        if static and a.n == 0:
                            dve.wait_ge(x0_loaded, 16)
                        else:
                            dve.wait_ge(x_loaded, 16)
                        statistics(a, 0, x_tile(a))
                    if s == MISC["shift1"] and bb.live():
                        split_lo(bb, 1)
                    if s == MISC["heads"] and cc.live():
                        dve.wait_ge(heads_ps, cc.n + 1)
                        heads = misc[:, :].rearrange("p (t h e) -> p t h e", t=NT, h=H)
                        dve.reciprocal(rden[:, :, :], heads[:, :, :, DK]).then_inc(rden_ready, 1)
                        dve.wait_ge(rden_ready, cc.n + 1)
                        dve.tensor_tensor(ctxn[:, :, :, :], heads[:, :, :, 0:DK],
                                          rden[:, :, :].rearrange("p t (h o) -> p t h o", o=1)
                                          .broadcast_to([P, NT, H, DK]), ALU.mult).then_inc(ctxn_ready, 1)
                    if s == 2 and a.live():
                        normalise(a, 0, x_tile(a), lambda t: xn[:, a.par, t, :], xn_ready)
                    if s == MISC["wo"] and cc.live():
                        dve.wait_ge(wo_ps, cc.n + 1)
                        dve.wait_ge(xbo_ready, cc.n + 1)
                        dve.tensor_tensor(x_batch(cc), misc[:, 0:S].rearrange("p (t d) -> p t d", t=NT),
                                          x_batch(cc), ALU.add).then_inc(x2_ready, 1)
                        wait_alone(dve, x2_ready, cc.n + 1)
                        statistics(cc, 1, x_tile(cc))
                    if s == 5 and cc.live():
                        normalise(cc, 1, x_tile(cc), lambda t: x2n[:, t, :], x2n_ready)
                    if s == MISC["qk"] and a.live():
                        dve.wait_ge(qk_hi_ready, 2 * a.n + 2)
                        for n, (w_c, hi, lo) in enumerate(((bq_c, q_hi, q_lo), (bk_c, k_hi, k_lo))):
                            dve.scalar_tensor_tensor(lo[:, a.par, :], misc[:, n * S:(n + 1) * S], w_c[:, :],
                                                     hi[:, a.par, :].bitcast(F32), op0=ALU.add,
                                                     op1=ALU.subtract).then_inc(qk_lo_ready, 1)
                    if s == MISC["x2T"] and cc.live():
                        dve.wait_ge(x2T_copy, 2 * cc.n + 2)
                        dve.tensor_tensor(x2T_lo[:, cc.par, :], misc[:, 0:S], x2T_hi[:, cc.par, :].bitcast(F32),
                                          ALU.subtract).then_inc(x2T_ready, 1)
                    if s == MISC["router"] and cc.live():
                        route(cc)
                    if s == MISC["v"] and m.live():
                        dve.wait_ge(v_ps, m.n + 1)
                        if static and m.n == 0:
                            dve.wait_ge(v_cols_ready, 1)
                        for j in range(2):
                            cols = slice(16 * j, 16 * j + DK)
                            ins = dve.tensor_tensor(
                                v_pad[:, m.par, :, :, :].rearrange("p t (k j) e -> p (t k) j e", j=2)[:, :, j, cols],
                                misc[:, 0:S].rearrange("p (a j d) -> p a j d", j=2, d=DK)[:, :, j, :],
                                bv_b[:, :, :].rearrange("p t (k j d) -> p (t k) j d", j=2, d=DK)[:, :, j, :],
                                ALU.add)
                        ins.then_inc(v_ready, 1)
                    if s == MISC["shift0"] and m.live():
                        split_lo(m, 0)
                if dd.live():
                    dve.wait_ge(out_ps, dd.n + 1)
                    dve.tensor_tensor(x_batch(dd), y_bank[:, 0:S].rearrange("p (t d) -> p t d", t=NT),
                                      x_batch(dd), ALU.add).then_inc(out_ready, 1)
                if static and i.n == 0:
                    key_rows(1)
                    dve.memset(v_pad[:, :, :, :, :], 0.0).then_inc(v_zero, 1)
                    dve.wait_ge(v_zero, 1)
                    ones = v_pad[:, :, :, :, :].rearrange("p b t (k j) e -> p (b t k) j e", j=2)
                    for j in range(2):
                        ins = dve.memset(ones[:, :, j, 16 * j + DK:16 * j + DK + 1], 1.0)
                    ins.then_inc(v_cols_ready, 1)
                if static and i.n == SETUP_STEP:
                    dve.wait_ge(w1_hi_ready, 1)
                    dve.tensor_tensor(w1_lo[:, :, :], w1_in[:, :, :], w1_hi[:, :, :].bitcast(F32), ALU.subtract)\
                       .then_inc(w1_ready, 1)
                    dve.wait_ge(w2_loaded, 16 * LOADS_W2)
                    dve.tensor_scalar(b1_neg[:, :], b1_in[:, :], -1.0, None, ALU.mult).then_inc(b1_neg_ready, 1)
                if static and i.n == SETUP_STEP + 1:
                    dve.wait_ge(setup_bias2, 1)
                    dve.tensor_tensor(bias2[:, :], misc[0:E, 0:D], b2_in[:, :], ALU.add).then_inc(bias2_ready, 1)

            steps(dve, one_step)

        @block.tensor
        def _(pe):
            taken = {"shift1": lambda b: (shift_lo[1], b.n + 1), "heads": lambda b: (ctxn_ready, b.n + 1),
                     "ctxT": lambda b: (ctxT_ready, b.n + 1), "wo": lambda b: (x2_ready, b.n + 1),
                     "inT": lambda b: (inT_ready, b.n + 1), "qk": lambda b: (qk_lo_ready, 2 * b.n + 2),
                     "x2T": lambda b: (x2T_ready, b.n + 1), "router": lambda b: (logits_ready, b.n + 1),
                     "v": lambda b: (v_ready, b.n + 1), "shift0": lambda b: (shift_lo[0], b.n + 1),
                     "cwT": lambda b: (cwT_ready, b.n + 1)}
            last_use = [None]

            def bank_taken():
                if last_use[0]:
                    name, b = last_use[0]
                    pe.wait_ge(*(taken[name](b) if name in taken else b))

            def transpose(dst, src):
                return pe.transpose(dst, src, ident[0:src.shape[0], 0:src.shape[0]])

            def misc_use(name, b):
                bank_taken()
                last_use[0] = (name, b)
                if name in ("shift0", "shift1"):
                    g = int(name[-1])
                    pe.wait_ge(negm_ready, H * b.n + HG * (g + 1))
                    for t in range(NT):
                        last = transpose(misc[0:HG, t * P:(t + 1) * P], negm[:, b.par, t, g * HG:(g + 1) * HG])
                    last.then_inc(shift_ps[g], 1)
                elif name == "heads":
                    pe.wait_ge(o_taken, b.n + 1)
                    for t in range(NT):
                        for g in range(2):
                            c = (t * 2 + g) * P
                            last = transpose(misc[:, c:c + P], oT[:, g, t * P:(t + 1) * P])
                    last.then_inc(heads_ps, 1)
                elif name == "ctxT":
                    pe.wait_ge(ctxn_ready, b.n + 1)
                    for t in range(NT):
                        last = transpose(misc[:, t * P:(t + 1) * P], ctxn[:, t, :, :].rearrange("p h d -> p (h d)"))
                    last.then_inc(ctxT_ps, 1)
                elif name == "wo":
                    pe.wait_ge(ctxT_ready, b.n + 1)
                    pe.wait_ge(wtail_loaded, 16 * LOADS_TAIL)
                    for t in range(NT):
                        last = pe.matmul(misc[:, t * P:(t + 1) * P], ctxT[:, t * P:(t + 1) * P], wo[:, :],
                                         start=True, stop=True)
                    last.then_inc(wo_ps, 1)
                elif name == "inT":
                    pe.wait_ge(xn_ready, NT * b.n + NT)
                    pe.wait_ge(c_cur_ready, b.n + 1)
                    for w, src in enumerate((xn, c_cur)):
                        for t in range(NT):
                            c = w * S + t * P
                            last = transpose(misc[:, c:c + P], src[:, b.par, t, :])
                    last.then_inc(inT_ps, 1)
                elif name == "qk":
                    pe.wait_ge(inT_ready, b.n + 1)
                    pe.wait_ge(wqkv_loaded, 16 * LOADS_QKV)
                    for n, w in enumerate((wq, wk)):
                        last = pe.matmul(misc[:, n * S:(n + 1) * S], w[:, :], inT[:, b.par, n, :],
                                         start=True, stop=True)
                    last.then_inc(qk_ps, 1)
                elif name == "v":
                    for t in range(NT):
                        last = pe.matmul(misc[:, t * P:(t + 1) * P], inT[:, b.par, 1, t * P:(t + 1) * P], wv[:, :],
                                         start=True, stop=True)
                    last.then_inc(v_ps, 1)
                elif name == "x2T":
                    pe.wait_ge(x2n_ready, NT * b.n + NT)
                    for t in range(NT):
                        last = transpose(misc[:, t * P:(t + 1) * P], x2n[:, t, :])
                    last.then_inc(x2T_ps, 1)
                elif name == "router":
                    pe.wait_ge(x2T_copy, 2 * b.n + 1)
                    for t in range(NT):
                        last = pe.matmul(misc[:, t * E:(t + 1) * E], x2T[:, t * P:(t + 1) * P], wr[:, :],
                                         start=True, stop=True)
                    last.then_inc(router_ps, 1)
                elif name == "cwT":
                    pe.wait_ge(cw_ready, b.n + 1)
                    for t in range(NT):
                        last = transpose(misc[0:E, t * P:(t + 1) * P], cw[:, t, :])
                    last.then_inc(cwT_ps, 1)

            def hidden(b, n):
                if n == 0:
                    pe.wait_ge(x2T_ready, b.n + 1)
                    pe.wait_ge(w1_ready, 1)
                z = z_bank[n % 2][:, 0:S]
                for k, (w, xT) in enumerate(((w1_hi, x2T_hi), (w1_hi, x2T_lo), (w1_lo, x2T_hi))):
                    last = pe.matmul(z, w[:, n, :], xT[:, b.par, :], start=k == 0, stop=k == 2)
                last.then_inc(z_ready, 1)

            def down(b, n):
                pe.wait_ge(g_ready, TILES * b.n + n + 1)
                last = pe.matmul(y_bank[:, 0:S], w2[:, n, :], g_t[:, n % G_BUFS, :], start=False,
                                 stop=n == TILES - 1)
                if n == TILES - 1:
                    last.then_inc(y_ready, 1)

            def values(b, q):
                pe.wait_ge(p_ready, H * b.n + 4 * q + 4)
                if q == 0:
                    pe.wait_ge(v_ready, b.n + 1)
                    if not isinstance(b.n, int) or b.n > 0:
                        pe.wait_ge(o_taken, b.n)
                g, j = q // 2, q % 2
                for k in range(NT):
                    for c in range(4):
                        n = 4 * q + c
                        last = pe.matmul(o_bank[32 * c:32 * c + 32, g, :], v_pad[:, b.par, k, head_of(n), :],
                                         probs[:, n % P_BUFS, k, :], start=j == 0 and k == 0,
                                         stop=j == 1 and k == NT - 1)
                last.then_inc(p_used, 1)

            def one_step(i):
                a, m, bb, cc, dd = (i.back(lag) for lag in (LAG_A, LAG_M, LAG_B, LAG_C, LAG_D))
                if not isinstance(i.n, int):
                    last_use[0] = None
                for s in range(SLOTS):
                    if bb.live():
                        h = head_of(s)
                        if s % HG == 0:
                            pe.wait_ge(shifts_in[s // HG], 16 * SHIFT_DMAS * (bb.n + 1))
                        if not isinstance(bb.n, int) or H * bb.n + s >= 2:
                            pe.wait_ge(p_ready, H * bb.n + s - 1)
                        for k in range(NT):
                            last = pe.matmul(s_bank[s % 2][:, k, :], Ks[bb.par][:, h, k * P:(k + 1) * P],
                                             Qs[bb.par][:, h, :], start=True, stop=True)
                        last.then_inc(s_ready, 1)
                    if dd.live():
                        if s == 0:
                            pe.wait_ge(cwT_ready, dd.n + 1)
                            pe.wait_ge(bias2_ready, 1)
                            pe.wait_ge(out_ready, dd.n + 1)
                            pe.matmul(y_bank[:, 0:S], bias2[:, :], cwT[:, dd.par, :], start=True, stop=False)
                        if s >= W2_LAG:
                            down(dd, s - W2_LAG)
                        hidden(dd, s)
                    if m.live():
                        if s % HG == 0:
                            pe.wait_ge(stacked[s // HG], 16 * STACK_DMAS * (m.n + 1))
                        if not isinstance(m.n, int) or H * m.n + s >= 1:
                            pe.wait_ge(negm_ready, H * m.n + s)
                        for t in range(NT):
                            last = pe.matmul(m_bank[:, t, :], Qs[m.par][:, s, t * P:(t + 1) * P],
                                             Ks[m.par][:, s, :], start=True, stop=True)
                        last.then_inc(m_ready, 1)
                    for name, slot in MISC.items():
                        b = i.back(MISC_LAG[name])
                        if slot == s and b.live():
                            misc_use(name, b)
                    if bb.live() and s in (5, 9, 13):
                        values(bb, s // 4 - 1)
                if dd.live():
                    for n in range(TILES - W2_LAG, TILES):
                        down(dd, n)
                if bb.live():
                    values(bb, 3)
                if dd.live():
                    pe.wait_ge(y_taken, dd.n + 1)
                    for t in range(NT):
                        last = transpose(y_bank[:, t * P:(t + 1) * P], yT[:, t * P:(t + 1) * P])
                    last.then_inc(out_ps, 1)
                if isinstance(i.n, int) and i.n == SETUP_STEP + 1:
                    bank_taken()
                    pe.wait_ge(b1_cols_ready, 1)
                    for n in range(TILES):
                        last = pe.matmul(misc[0:E, 0:D], b1_cols[:, n, :], w2[:, n, :], start=n == 0,
                                         stop=n == TILES - 1)
                    last.then_inc(setup_bias2, 1)
                    last_use[0] = ("setup", (bias2_ready, 1))

            pe.wait_ge(ident_step, 2)
            steps(pe, one_step)


_INS = ['x', 'ctx_1024', 'L0_xattn_Wq', 'L0_xattn_bq', 'L0_xattn_Wk', 'L0_xattn_bk', 'L0_xattn_Wv', 'L0_xattn_bv',
        'L0_xattn_Wo', 'L0_xattn_bo', 'L0_ffn_Wr', 'L0_ffn_br', 'L0_ffn_W1', 'L0_ffn_b1', 'L0_ffn_W2', 'L0_ffn_b2']


def _laid_out(name, a):
    if name in ('x', 'ctx_1024'):
        return a.reshape(B * NT, P, D).transpose(1, 0, 2)
    if name in ('L0_xattn_Wq', 'L0_xattn_Wk', 'L0_xattn_bq', 'L0_xattn_bk'):
        a = a.reshape(-1, 2, HG, DK).transpose(0, 1, 3, 2).reshape(-1, D)
        return a if len(a) > 1 else a.reshape(D, 1)
    if name in ('L0_xattn_bv', 'L0_xattn_bo', 'L0_ffn_br'):
        return a.reshape(1, -1)
    if name == 'L0_ffn_W1':
        return a.transpose(1, 0, 2).reshape(D, TILES, P)
    if name == 'L0_ffn_W2':
        return a.reshape(TILES, P, D).transpose(1, 0, 2)
    if name == 'L0_ffn_b1':
        return a.reshape(TILES, P).transpose(1, 0)
    return a


def kernel(**inputs):
    import numpy as _np
    import concourse.bacc as _bacc
    from concourse import mybir as _mybir
    from concourse.bass_utils import run_bass_kernel_spmd as _run

    nc = _bacc.Bacc("TRN2", target_bir_lowering=False, num_devices=1)
    arrays, args = {}, []
    for name in _INS:
        a = _np.ascontiguousarray(_laid_out(name, _np.asarray(inputs[name])))
        arrays[f"in_{name}_dram"] = a
        args.append(nc.dram_tensor(f"in_{name}_dram", a.shape, _mybir.dt.from_np(a.dtype), kind="ExternalInput").ap())
    args.append(nc.dram_tensor("out_0_dram", (P, B * NT, D), F32, kind="ExternalOutput").ap())
    xattn_moe(nc, *args)
    r = _run(nc, [arrays], core_ids=[0])
    got = _np.asarray(r.results[0]["out_0_dram"])
    return _np.ascontiguousarray(got.transpose(1, 0, 2)).reshape(B, S, D)
```

```python
import concourse.bass as bass
from concourse import mybir
from contextlib import ExitStack

F32 = mybir.dt.float32
F32R = mybir.dt.float32r
U32 = mybir.dt.uint32
ALU = mybir.AluOpType
ACT = mybir.ActivationFunctionType
AX = mybir.AxisListType

B, S, D = 8, 256, 128
H, DK = 16, 8
E, DF = 8, 256
P = 128
NT = S // P
TILES = E * DF // P
HG = 8
SHIFT_ROW = 4 * DK
EPS = 1e-5
EXP_SCALE = float(DK) ** -0.5
P_BUFS = 8
G_BUFS = 4
W2_LAG = 4
SLOTS = 16

LAG_A, LAG_M, LAG_B, LAG_C, LAG_D = 0, 1, 2, 3, 4
STEPS = B + LAG_D
MISC = {"heads": 1, "ctxT": 2, "wo": 3, "inT": 5, "x2T": 6, "router": 7, "qk": 8, "cwT": 10,
        "shift0": 11, "v": 12}
LN1_STATS, LN1_OUT, LN2_OUT, QK_LO = 2, 4, 5, 9
VALUES = {5: (0, 0), 7: (0, 1), 8: (1, 0), 9: (1, 1), 12: (2, 0), 13: (2, 1)}
MISC_LAG = {"shift1": LAG_M, "heads": LAG_C, "ctxT": LAG_C, "wo": LAG_C, "inT": LAG_A, "qk": LAG_A,
            "x2T": LAG_C, "router": LAG_C, "v": LAG_M, "shift0": LAG_M, "cwT": LAG_C}
BIAS2_SLOT = 8
SETUP_STEP, BIAS_FROM = 1, 12
LOADS_QK, LOADS_V, LOADS_W2, LOADS_TAIL = 4, 2, 3, 4
PARTS_DMAS = 8
ROUTE_CHAIN = 8


class Batch:

    def __init__(self, t, c):
        self.t, self.c = t, c
        self.n = 2 * t + c
        self.par = c % 2

    def back(self, lag):
        return Batch(self.t, self.c - lag)

    def live(self):
        return not isinstance(self.n, int) or 0 <= self.n < B


def stack_dmas(n):
    return PARTS_DMAS * n + (max(n - 2, 0) if isinstance(n, int) else n - 2)


def head_of(n):
    g, j, c = n // HG, n // 4 % 2, n % 4
    return g * HG + c * 2 + j


def wait_alone(eng, semaphore, value):
    if not isinstance(value, int):
        value = eng.to_reg(value)
        eng.wait_ge(semaphore, 1)
    eng.wait_ge(semaphore, value)


def steps(eng, one_step):
    first, last = LAG_D, B
    for c in range(first):
        one_step(Batch(0, c))
    with eng.Fori(first // 2, last // 2) as t:
        one_step(Batch(t, 0))
        one_step(Batch(t, 1))
    for c in range(last, STEPS):
        one_step(Batch(0, c))


def xattn_moe(nc, x, ctx_in, Wq, bq, Wk, bk, Wv, bv, Wo, bo, Wr, br, W1, b1, W2, b2, out):
    es = ExitStack()
    with es:
        def sb(name, shape, dt=F32):
            return es.enter_context(nc.sbuf_tensor(name, shape, dt))

        def ps(name, shape):
            return es.enter_context(nc.psum_tensor(name, shape, F32))

        def sem(name):
            return es.enter_context(nc.semaphore(name))

        x_all = sb("x_all", [P, B * NT, D])
        c_cur = sb("c_cur", [P, 2, NT, D])
        xn = sb("xn", [P, 2, NT, D])
        inT = sb("inT", [P, 2, 2, S])
        q_whole = sb("q_whole", [P, S])
        k_whole = sb("k_whole", [P, S])
        q_hi = sb("q_hi", [P, 2, S], F32R)
        q_lo = sb("q_lo", [P, 2, S], F32R)
        k_hi = sb("k_hi", [P, 2, S], F32R)
        k_lo = sb("k_lo", [P, 2, S], F32R)
        Qs = [sb(f"Qs{n}", [P, H, S], F32R) for n in range(2)]
        Ks = [sb(f"Ks{n}", [P, H, S], F32R) for n in range(2)]
        v_pad = sb("v_pad", [P, 2, NT, H, 32])
        negm = sb("negm", [P, 2, NT, H])
        negm_parts = sb("negm_parts", [P, 2, NT, 2, HG], F32R)
        shift_rows = sb("shift_rows", [2 * HG, 2, S], F32R)
        zero_rows = sb("zero_rows", [2 * HG, S])
        probs = sb("probs", [P, P_BUFS, NT, S])
        oT = sb("oT", [P, 2, S])
        rden = sb("rden", [P, NT, H])
        ctxn = sb("ctxn", [P, NT, H, DK])
        ctxT = sb("ctxT", [P, S])
        stats = sb("stats", [P, 2, NT, 6])
        mv = sb("mv", [P, 2, NT, 2])
        rstd = sb("rstd", [P, 2, NT])
        var_eps = sb("var_eps", [P, 2, NT])
        neg_mean = sb("neg_mean", [P, 2, NT])
        nmr = sb("nmr", [P, 2, NT])
        minus_one = sb("minus_one", [P, NT])
        x2n = sb("x2n", [P, NT, D])
        x2T = sb("x2T", [P, S])
        x2T_hi = sb("x2T_hi", [P, 2, S], F32R)
        x2T_lo = sb("x2T_lo", [P, 2, S], F32R)
        logits = sb("logits", [P, NT, E])
        top = sb("top", [P, NT, 8])
        top_i = sb("top_i", [P, NT, 8], U32)
        top_f = sb("top_f", [P, NT, 8])
        shifted = sb("shifted", [P, NT, E])
        pexp = sb("pexp", [P, NT, E])
        psum_e = sb("psum_e", [P, NT])
        rsum_e = sb("rsum_e", [P, NT])
        pick1 = sb("pick1", [P, NT, E])
        pick2 = sb("pick2", [P, NT, E])
        picked = sb("picked", [P, NT, E])
        cw = sb("cw", [P, NT, E])
        cwT = sb("cwT", [E, 2, S])
        cw_b = sb("cw_b", [P, 2, E, S])
        g_t = sb("g_t", [P, G_BUFS, S])
        g_hi = sb("g_hi", [P, G_BUFS, S], F32R)
        g_lo = sb("g_lo", [P, G_BUFS, S], F32R)
        yT = sb("yT", [P, S])
        ident = sb("ident", [P, P])
        empty_turn = sb("empty_turn", [P, 1])
        eps = sb("eps", [P, NT])
        half = sb("half", [P, NT])
        expert_no = sb("expert_no", [P, E])
        wq = sb("wq", [P, D])
        wk = sb("wk", [P, D])
        wv = sb("wv", [P, D])
        wo = sb("wo", [P, D])
        wr = sb("wr", [P, E])
        bq_c = sb("bq_c", [P, 1])
        bk_c = sb("bk_c", [P, 1])
        bv_b = sb("bv_b", [P, 1, D])
        bo_b = sb("bo_b", [P, 1, D])
        br_b = sb("br_b", [P, 1, E])
        w1_hi = sb("w1_hi", [P, TILES, P], F32R)
        w1_lo = sb("w1_lo", [P, TILES, P], F32R)
        w2_hi = sb("w2_hi", [P, TILES, P], F32R)
        w2_lo = sb("w2_lo", [P, TILES, P], F32R)
        w1_in, w2_in = (cw_b[:, n, :, :].rearrange("p e s -> p (e s)").rearrange("p (n d) -> p n d", d=P)
                        for n in range(2))
        b1_in = sb("b1_in", [P, TILES])
        b1_neg = sb("b1_neg", [P, TILES])
        b1_cols = sb("b1_cols", [P, TILES, E])
        b2_in = sb("b2_in", [E, D])
        bias2 = sb("bias2", [E, D])

        s_bank = [ps(f"s_bank{n}", [P, NT, S]) for n in range(2)]
        o_bank = ps("o_bank", [P, 2, S])
        turn_banks = [ps(f"turn_bank{n}", [P, 512]) for n in range(3)]
        y_bank = ps("y_bank", [P, 512])
        misc = ps("misc", [P, 512])

        cw_dram = nc.dram_tensor("cw_scratch", (2, E, S), F32, kind="Internal").ap()

        x0_loaded = sem("x0_loaded")
        x_loaded = sem("x_loaded")
        c_loaded = sem("c_loaded")
        wqk_loaded = sem("wqk_loaded")
        wv_loaded = sem("wv_loaded")
        wtail_loaded = sem("wtail_loaded")
        w1_loaded = sem("w1_loaded")
        w2_loaded = sem("w2_loaded")
        const_ready = sem("const_ready")
        ident_step = sem("ident_step")
        w_hi_ready = sem("w_hi_ready")
        w_lo_ready = sem("w_lo_ready")
        q_rows_ready = sem("q_rows_ready")
        k_rows_ready = sem("k_rows_ready")
        v_zero = sem("v_zero")
        v_cols_ready = sem("v_cols_ready")
        b1_neg_ready = sem("b1_neg_ready")
        b1_cols_ready = sem("b1_cols_ready")
        bias2_ready = sem("bias2_ready")
        setup_bias2 = sem("setup_bias2")
        stat_ready = [sem("ln1_stat_ready"), sem("ln2_stat_ready")]
        aggr_ready = [sem("ln1_aggr_ready"), sem("ln2_aggr_ready")]
        vareps_ready = [sem("ln1_vareps_ready"), sem("ln2_vareps_ready")]
        rstd_ready = [sem("ln1_rstd_ready"), sem("ln2_rstd_ready")]
        nmr_ready = [sem("ln1_nmr_ready"), sem("ln2_nmr_ready")]
        xn_ready = sem("xn_ready")
        xbo_ready = sem("xbo_ready")
        inT_ps = sem("inT_ps")
        inT_ready = sem("inT_ready")
        qk_ps = sem("qk_ps")
        qk_hi_ready = sem("qk_hi_ready")
        qk_whole_ready = sem("qk_whole_ready")
        qk_lo_ready = sem("qk_lo_ready")
        v_ps = sem("v_ps")
        v_ready = sem("v_ready")
        stacked = [sem("stacked0"), sem("stacked1")]
        m_ready = sem("m_ready")
        negm_ready = sem("negm_ready")
        shift_ps = [sem("shift0_ps"), sem("shift1_ps")]
        parts_hi = [sem("parts0_hi"), sem("parts1_hi")]
        parts_ready = [sem("parts0_ready"), sem("parts1_ready")]
        shift_ready = [sem("shift0_ready"), sem("shift1_ready")]
        shifts_in = [sem("shift0_in"), sem("shift1_in")]
        s_ready = sem("s_ready")
        p_ready = sem("p_ready")
        p_used = sem("p_used")
        o_taken = sem("o_taken")
        heads_ps = sem("heads_ps")
        rden_ready = sem("rden_ready")
        ctxn_ready = sem("ctxn_ready")
        ctxT_ps = sem("ctxT_ps")
        ctxT_ready = sem("ctxT_ready")
        wo_ps = sem("wo_ps")
        x2_ready = sem("x2_ready")
        x2n_ready = sem("x2n_ready")
        x2T_ps = sem("x2T_ps")
        x2T_copy = sem("x2T_copy")
        x2T_ready = sem("x2T_ready")
        router_ps = sem("router_ps")
        logits_ready = sem("logits_ready")
        route_step = sem("route_step")
        shifted_ready = sem("shifted_ready")
        pexp_ready = sem("pexp_ready")
        cw_ready = sem("cw_ready")
        cwT_ps = sem("cwT_ps")
        cwT_ready = sem("cwT_ready")
        cw_stored = sem("cw_stored")
        cw_b_ready = sem("cw_b_ready")
        z_ready = sem("z_ready")
        g_ready = sem("g_ready")
        g_hi_ready = sem("g_hi_ready")
        g_lo_ready = sem("g_lo_ready")
        y_ready = sem("y_ready")
        y_taken = sem("y_taken")
        out_ps = sem("out_ps")
        out_ready = sem("out_ready")
        stored = sem("stored")

        block = es.enter_context(nc.Block())

        def turn_bank(n):
            return turn_banks[n % 3]

        def hidden_bank(n, m):
            return turn_bank(2 * n if m.live() else n)[:, 0:S]

        def scores_bank(h, d):
            return turn_bank(2 * h + 1 if d.live() else h)[:, :].rearrange("p (t s) -> p t s", t=NT)

        @block.sync
        def _(sp):
            sp.dma_start(x_all[:, 0:NT, :], x[:, 0:NT, :]).then_inc(x0_loaded, 16)
            sp.dma_start(c_cur[:, 0, :, :], ctx_in[:, 0:NT, :]).then_inc(c_loaded, 16)
            sp.dma_start(wq[:, :], Wq).then_inc(wqk_loaded, 16)
            sp.dma_start(wk[:, :], Wk).then_inc(wqk_loaded, 16)
            sp.dma_start(bq_c[:, :], bq).then_inc(wqk_loaded, 16)
            sp.dma_start(bk_c[:, :], bk).then_inc(wqk_loaded, 16)
            sp.dma_start(x_all[:, NT:, :], x[:, NT:, :]).then_inc(x_loaded, 16)
            sp.dma_start(wv[:, :], Wv).then_inc(wv_loaded, 16)
            sp.dma_start(bv_b[:, 0, :], bv.broadcast_to([P, D])).then_inc(wv_loaded, 16)
            sp.dma_start(bo_b[:, 0, :], bo.broadcast_to([P, D])).then_inc(wtail_loaded, 16)
            sp.dma_start(br_b[:, 0, :], br.broadcast_to([P, E])).then_inc(wtail_loaded, 16)
            sp.dma_start(wo[:, :], Wo).then_inc(wtail_loaded, 16)
            sp.dma_start(wr[:, :], Wr).then_inc(wtail_loaded, 16)
            sp.dma_start(w1_in, W1).then_inc(w1_loaded, 16)
            sp.dma_start(w2_in, W2).then_inc(w2_loaded, 16)
            sp.dma_start(b1_in[:, :], b1).then_inc(w2_loaded, 16)
            sp.dma_start(b2_in[:, :], b2).then_inc(w2_loaded, 16)

            def stack(b, g, bb):
                heads = slice(HG * g, HG * (g + 1))
                rows = slice(64 * g, 64 * g + 64)
                his, los, scores = 2 * b.n + 2, 2 * b.n + 2, H * bb.n + HG * (g + 1)
                if not isinstance(b.n, int):
                    his, los, scores = sp.to_reg(his), sp.to_reg(los), sp.to_reg(scores)
                if bb.live():
                    sp.wait_ge(s_ready, scores)
                if isinstance(b.n, int) and b.n < 2:
                    sp.wait_ge(q_rows_ready, 2 * b.n + g + 1)
                    sp.wait_ge(k_rows_ready, 2 * b.n + g + 1)
                sp.wait_ge(qk_hi_ready, his)
                for r, dst, src in ((0, Qs, q_hi), (0, Ks, k_hi), (1, Qs, q_hi), (2, Ks, k_hi),
                                    (2, Qs, q_lo), (1, Ks, k_lo), (3, Qs, q_lo), (3, Ks, k_lo)):
                    if r == 2 and src is q_lo:
                        sp.wait_ge(qk_lo_ready, los)
                    sp.dma_start(dst[b.par][DK * r:DK * (r + 1), heads, :].bitcast(F32),
                                 src[rows, b.par, :].bitcast(F32)).then_inc(stacked[g], 16)
                if not isinstance(b.n, int) or b.n >= 2:
                    sp.dma_start(Qs[b.par][SHIFT_ROW:SHIFT_ROW + 2, heads, :].bitcast(F32), zero_rows[:, :])\
                      .then_inc(stacked[g], 16)

            def shift(b, g):
                heads = slice(HG * g, HG * (g + 1))
                sp.wait_ge(shift_ready[g], b.n + 1)
                sp.dma_start(Qs[b.par][SHIFT_ROW:SHIFT_ROW + 2, heads, :].bitcast(F32),
                             shift_rows[:, g, :].bitcast(F32)).then_inc(shifts_in[g], 16)

            def one_step(i):
                a, m, bb, cc, dd = (i.back(lag) for lag in (LAG_A, LAG_M, LAG_B, LAG_C, LAG_D))
                if a.live() and not (isinstance(a.n, int) and a.n == 0):
                    sp.dma_start(c_cur[:, a.par, :, :], ctx_in[:, bass.ds(NT * a.n, NT), :])\
                      .then_inc(c_loaded, 16)
                if a.live():
                    stack(a, 0, bb)
                if isinstance(i.n, int) and i.n == 0:
                    stack(a, 1, bb)
                if m.live():
                    shift(m, 0)
                if a.live() and not (isinstance(i.n, int) and i.n == 0):
                    stack(a, 1, bb)
                if m.live():
                    shift(m, 1)
                if dd.live():
                    wait_alone(sp, out_ready, dd.n + 2)
                    sp.dma_start(out[:, bass.ds(NT * dd.n, NT), :],
                                 x_all[:, bass.ds(NT * dd.n, NT), :]).then_inc(stored, 16)

            steps(sp, one_step)
            sp.wait_ge(stored, 16 * B)

        @block.gpsimd
        def _(pool):
            pool.memset(ident[:, :], 0.0).then_inc(ident_step, 1)
            pool.wait_ge(ident_step, 1)
            pool.affine_select(out=ident[:, :], in_=ident[:, :], compare_op=ALU.not_equal, fill=1.0,
                               base=0, pattern=[[-1, P]], channel_multiplier=1).then_inc(ident_step, 1)
            pool.memset(half[:, :], -0.5)
            pool.memset(minus_one[:, :], -1.0)
            pool.memset(eps[:, :], EPS)
            for e in range(E):
                last = pool.memset(expert_no[:, e:e + 1], float(e))
            last.then_inc(const_ready, 1)

            def query_rows(n):
                for g in range(2):
                    pool.memset(Qs[n][:, HG * g:HG * (g + 1), :].bitcast(F32), 0.0).then_inc(q_rows_ready, 1)

            def inverse_root(b, ln):
                pool.wait_ge(aggr_ready[ln], NT * b.n + NT)
                pool.tensor_tensor(neg_mean[:, ln, :], mv[:, ln, :, 0], minus_one[:, :], ALU.mult)
                pool.tensor_tensor(var_eps[:, ln, :], mv[:, ln, :, 1], eps[:, :], ALU.add)\
                    .then_inc(vareps_ready[ln], 1)
                pool.wait_ge(vareps_ready[ln], b.n + 1)
                pool.tensor_tensor(rstd[:, ln, :], var_eps[:, ln, :], half[:, :], ALU.pow)\
                    .then_inc(rstd_ready[ln], 1)
                pool.wait_ge(rstd_ready[ln], b.n + 1)
                pool.tensor_tensor(nmr[:, ln, :], neg_mean[:, ln, :], rstd[:, ln, :], ALU.mult)\
                    .then_inc(nmr_ready[ln], 1)

            def prepare_experts(k):
                if k == 0:
                    pool.wait_ge(w2_loaded, 16 * LOADS_W2)
                    pool.wait_ge(const_ready, 2)
                    for e in range(E):
                        last = pool.tensor_copy(b1_cols[:, 2 * e:2 * e + 2, e], b1_in[:, 2 * e:2 * e + 2])
                    last.then_inc(b1_cols_ready, 1)
                else:
                    pool.wait_ge(setup_bias2, 1)
                w_lo, w_in, w_hi = ((w1_lo, w1_in, w1_hi), (w2_lo, w2_in, w2_hi))[k]
                pool.wait_ge(w_hi_ready, k + 1)
                pool.tensor_tensor(w_lo[:, :, :], w_in, w_hi[:, :, :].bitcast(F32), ALU.subtract)\
                    .then_inc(w_lo_ready, 1)

            def one_step(i):
                a, cc, dd = (i.back(lag) for lag in (LAG_A, LAG_C, LAG_D))
                if isinstance(i.n, int) and i.n == 0:
                    inverse_root(a, 0)
                    query_rows(0)
                if isinstance(i.n, int) and i.n == 0:
                    query_rows(1)
                    pool.memset(zero_rows[:, :], 0.0)
                    pool.memset(b1_cols[:, :, :], 0.0).then_inc(const_ready, 1)
                for s in range(SLOTS):
                    if dd.live():
                        pool.wait_ge(g_hi_ready, TILES * dd.n + s + 1)
                        pool.tensor_tensor(g_lo[:, s % G_BUFS, :], g_t[:, s % G_BUFS, :],
                                           g_hi[:, s % G_BUFS, :].bitcast(F32), ALU.subtract)\
                            .then_inc(g_lo_ready, 1)
                    if s == LN1_STATS and a.live() and not (isinstance(a.n, int) and a.n == 0):
                        inverse_root(a, 0)
                    if s == MISC["wo"] and cc.live():
                        inverse_root(cc, 1)
                    if s == QK_LO and a.live():
                        pool.wait_ge(qk_whole_ready, 2 * a.n + 2)
                        for whole, hi, lo in ((q_whole, q_hi, q_lo), (k_whole, k_hi, k_lo)):
                            pool.tensor_tensor(lo[:, a.par, :], whole[:, :], hi[:, a.par, :].bitcast(F32),
                                               ALU.subtract).then_inc(qk_lo_ready, 1)
                    if s == QK_LO and a.live():
                        pool.wait_ge(wtail_loaded, 16 * LOADS_TAIL)
                        pool.wait_ge(xn_ready, NT * a.n + NT)
                        xb = x_all[:, bass.ds(NT * a.n, NT), :]
                        pool.tensor_tensor(xb, xb, bo_b[:, :, :].broadcast_to([P, NT, D]), ALU.add)\
                            .then_inc(xbo_ready, 1)
                    if s == QK_LO and isinstance(i.n, int) and i.n in (SETUP_STEP, SETUP_STEP + 1):
                        prepare_experts(i.n - SETUP_STEP)
                    if s == MISC["x2T"] and cc.live():
                        pool.wait_ge(x2T_copy, 2 * cc.n + 2)
                        pool.tensor_tensor(x2T_lo[:, cc.par, :], x2T[:, :], x2T_hi[:, cc.par, :].bitcast(F32),
                                           ALU.subtract).then_inc(x2T_ready, 1)

            pool.wait_ge(const_ready, 1)
            steps(pool, one_step)

        @block.scalar
        def _(act):
            def normalise(b, ln, dst, done):
                act.wait_ge(nmr_ready[ln], b.n + 1)
                for t in range(NT):
                    act.activation(dst[:, t, :], x_all[:, bass.ds(NT * b.n + t, 1), :], ACT.Identity,
                                   bias=nmr[:, ln, t:t + 1], scale=rstd[:, ln, t:t + 1]).then_inc(done, 1)

            def take_shift(b, g):
                act.wait_ge(shift_ps[g], b.n + 1)
                act.activation(shift_rows[:, g, :], misc[0:2 * HG, 0:S], ACT.Copy).then_inc(shift_ready[g], 1)

            def one_step(i):
                a, m, bb, cc, dd = (i.back(lag) for lag in (LAG_A, LAG_M, LAG_B, LAG_C, LAG_D))
                if isinstance(i.n, int) and i.n == SETUP_STEP:
                    act.wait_ge(w1_loaded, 16)
                    act.activation(w1_hi[:, :, :], w1_in, ACT.Copy).then_inc(w_hi_ready, 1)
                    act.wait_ge(w2_loaded, 16 * LOADS_W2)
                    act.activation(w2_hi[:, :, :], w2_in, ACT.Copy).then_inc(w_hi_ready, 1)
                for s in range(SLOTS):
                    if bb.live():
                        n = H * bb.n + s
                        act.wait_ge(s_ready, n + 1)
                        if s % 4 == 0 and (not isinstance(bb.n, int) or bb.n > 0 or s >= P_BUFS):
                            act.wait_ge(p_used, 4 * bb.n + s // 4 + 1 - P_BUFS // 4)
                        act.activation(probs[:, s % P_BUFS, :, :], s_bank[s % 2][:, :, :], ACT.Exp,
                                       scale=EXP_SCALE).then_inc(p_ready, 1)
                    if dd.live():
                        act.wait_ge(g_ready, TILES * dd.n + s + 1)
                        act.activation(g_hi[:, s % G_BUFS, :], g_t[:, s % G_BUFS, :], ACT.Copy)\
                           .then_inc(g_hi_ready, 1)
                    if s == LN1_OUT and a.live():
                        normalise(a, 0, xn[:, a.par, :, :], xn_ready)
                    if s == LN2_OUT and cc.live():
                        normalise(cc, 1, x2n, x2n_ready)
                    if s == MISC["ctxT"] and cc.live():
                        act.wait_ge(ctxT_ps, cc.n + 1)
                        act.activation(ctxT[:, :], misc[:, 0:S], ACT.Copy).then_inc(ctxT_ready, 1)
                    if s == MISC["inT"] and a.live():
                        act.wait_ge(inT_ps, a.n + 1)
                        act.activation(inT[:, a.par, :, :], misc[:, :].rearrange("p (w t) -> p w t", w=2),
                                       ACT.Copy).then_inc(inT_ready, 1)
                    if s == MISC["qk"] and a.live():
                        act.wait_ge(qk_ps, a.n + 1)
                        act.activation(q_hi[:, a.par, :], misc[:, 0:S], ACT.Identity, bias=bq_c[:, :])\
                           .then_inc(qk_hi_ready, 1)
                        act.activation(k_hi[:, a.par, :], misc[:, S:2 * S], ACT.Identity, bias=bk_c[:, :])\
                           .then_inc(qk_hi_ready, 1)
                        act.activation(q_whole[:, :], misc[:, 0:S], ACT.Identity, bias=bq_c[:, :])\
                           .then_inc(qk_whole_ready, 1)
                        act.activation(k_whole[:, :], misc[:, S:2 * S], ACT.Identity, bias=bk_c[:, :])\
                           .then_inc(qk_whole_ready, 1)
                    if s == MISC["x2T"] and cc.live():
                        act.wait_ge(x2T_ps, cc.n + 1)
                        act.activation(x2T[:, :], misc[:, 0:S], ACT.Copy).then_inc(x2T_copy, 1)
                        act.activation(x2T_hi[:, cc.par, :], misc[:, 0:S], ACT.Copy).then_inc(x2T_copy, 1)
                    if s == MISC["router"] + 1 and cc.live():
                        act.wait_ge(shifted_ready, cc.n + 1)
                        act.activation(pexp[:, :, :], shifted[:, :, :], ACT.Exp).then_inc(pexp_ready, 1)
                    if s == MISC["shift0"] and m.live():
                        take_shift(m, 0)
                    if s == MISC["cwT"] and cc.live():
                        act.wait_ge(cwT_ps, cc.n + 1)
                        act.activation(cwT[:, cc.par, :], misc[0:E, 0:S], ACT.Copy).then_inc(cwT_ready, 1)
                        if not isinstance(cc.n, int) or cc.n >= 2:
                            act.wait_ge(cw_b_ready, 16 * cc.n - 16)
                        act.wait_ge(cwT_ready, cc.n + 1)
                        act.dma_start(cw_dram[cc.par], cwT[:, cc.par, :]).then_inc(cw_stored, 16)
                    if s == MISC["cwT"] + 2 and cc.live():
                        if isinstance(cc.n, int) and cc.n == 0:
                            act.wait_ge(w_lo_ready, 2)
                        act.wait_ge(cw_stored, 16 * cc.n + 16)
                        act.dma_start(cw_b[:, cc.par, :, :],
                                      cw_dram[cc.par:cc.par + 1].broadcast_to([P, E, S])).then_inc(cw_b_ready, 16)
                if dd.live():
                    act.wait_ge(y_ready, dd.n + 1)
                    act.activation(yT[:, :], y_bank[:, 0:S], ACT.Copy).then_inc(y_taken, 1)
                if m.live():
                    take_shift(m, 1)
                if bb.live():
                    act.wait_ge(p_used, 4 * bb.n + 4)
                    act.activation(oT[:, :, :], o_bank[:, :, :], ACT.Copy).then_inc(o_taken, 1)

            steps(act, one_step)

        @block.vector
        def _(dve):
            def key_rows(n):
                for g in range(2):
                    heads = slice(HG * g, HG * (g + 1))
                    dve.memset(Ks[n][:, heads, :].bitcast(F32), 1.0).then_inc(k_rows_ready, 1)

            dve.memset(empty_turn[:, :], 0.0).then_inc(out_ready, 1)

            def statistics(b, ln, src):
                for t in range(NT):
                    last = dve.bn_stats(stats[:, ln, t, :], src(t))
                last.then_inc(stat_ready[ln], 1)
                wait_alone(dve, stat_ready[ln], b.n + 1)
                for t in range(NT):
                    dve.bn_aggr(mv[:, ln, t, :], stats[:, ln, t, :]).then_inc(aggr_ready[ln], 1)

            def split_maxima(b, g):
                whole = negm[:, b.par, :, HG * g:HG * (g + 1)]
                wait_alone(dve, negm_ready, H * b.n + HG * (g + 1))
                dve.tensor_copy(negm_parts[:, g, :, 0, :], whole).then_inc(parts_hi[g], 1)
                dve.wait_ge(parts_hi[g], b.n + 1)
                dve.tensor_tensor(negm_parts[:, g, :, 1, :], whole, negm_parts[:, g, :, 0, :].bitcast(F32),
                                  ALU.subtract).then_inc(parts_ready[g], 1)

            def x_tile(b):
                return lambda t: x_all[:, bass.ds(NT * b.n + t, 1), :]

            def x_batch(b):
                return x_all[:, bass.ds(NT * b.n, NT), :]

            links = [0]

            def link(b, ins):
                links[0] += 1
                ins.then_inc(route_step, 1)
                dve.wait_ge(route_step, ROUTE_CHAIN * b.n + links[0])

            def rank(b):
                links[0] = 0
                dve.wait_ge(router_ps, b.n + 1)
                dve.tensor_tensor(logits[:, :, :], misc[:, 0:NT * E].rearrange("p (t e) -> p t e", t=NT),
                                  br_b[:, :, :].broadcast_to([P, NT, E]), ALU.add).then_inc(logits_ready, 1)
                wait_alone(dve, logits_ready, b.n + 1)
                dve.max(out=top[:, 0, :], in_=logits[:, 0, :])
                link(b, dve.max(out=top[:, 1, :], in_=logits[:, 1, :]))
                dve.tensor_tensor(shifted[:, :, :], logits[:, :, :], top[:, :, 0:1].broadcast_to([P, NT, E]),
                                  ALU.subtract).then_inc(shifted_ready, 1)
                dve.max_index(top_i[:, 0, :], top[:, 0, :], logits[:, 0, :])
                link(b, dve.max_index(top_i[:, 1, :], top[:, 1, :], logits[:, 1, :]))
                link(b, dve.tensor_copy(top_f[:, :, :], top_i[:, :, :]))

            def combine_weights(b):
                dve.wait_ge(pexp_ready, b.n + 1)
                link(b, dve.tensor_reduce(psum_e[:, :], pexp[:, :, :], AX.X, ALU.add))
                link(b, dve.reciprocal(rsum_e[:, :], psum_e[:, :]))
                for t in range(NT):
                    for pick, k in ((pick1, 0), (pick2, 1)):
                        ins = dve.scalar_tensor_tensor(pick[:, t, :], expert_no[:, :], top_f[:, t, k:k + 1],
                                                       pexp[:, t, :], op0=ALU.is_equal, op1=ALU.mult)
                        if k == 1:
                            link(b, ins)
                link(b, dve.tensor_tensor(picked[:, :, :], pick1[:, :, :], pick2[:, :, :], ALU.add))
                dve.tensor_tensor(cw[:, :, :], picked[:, :, :],
                                  rsum_e[:, :].rearrange("p (t o) -> p t o", o=1).broadcast_to([P, NT, E]),
                                  ALU.mult).then_inc(cw_ready, 1)
                assert links[0] == ROUTE_CHAIN

            def one_step(i):
                a, m, bb, cc, dd = (i.back(lag) for lag in (LAG_A, LAG_M, LAG_B, LAG_C, LAG_D))
                static = isinstance(i.n, int)
                for s in range(SLOTS):
                    if dd.live():
                        dve.wait_ge(z_ready, TILES * dd.n + s + 1)
                        if s == 0:
                            dve.wait_ge(cw_b_ready, 16 * dd.n + 16)
                        dve.scalar_tensor_tensor(g_t[:, s % G_BUFS, :], hidden_bank(s, m), b1_neg[:, s:s + 1],
                                                 cw_b[:, dd.par, s // 2, :], op0=ALU.max, op1=ALU.mult)\
                           .then_inc(g_ready, 1)
                    if m.live():
                        dve.wait_ge(m_ready, H * m.n + s + 1)
                        dve.tensor_reduce(negm[:, m.par, :, s], scores_bank(s, dd), AX.X, ALU.max, negate=True)\
                           .then_inc(negm_ready, 1)
                        if s % HG == HG - 1:
                            split_maxima(m, s // HG)
                    if s == LN1_STATS and a.live():
                        if static and a.n == 0:
                            dve.wait_ge(x0_loaded, 16)
                        else:
                            dve.wait_ge(x_loaded, 16)
                        statistics(a, 0, x_tile(a))
                    if s == MISC["heads"] and cc.live():
                        dve.wait_ge(heads_ps, cc.n + 1)
                        heads = misc[:, :].rearrange("p (t h e) -> p t h e", t=NT, h=H)
                        dve.reciprocal(rden[:, :, :], heads[:, :, :, DK]).then_inc(rden_ready, 1)
                        dve.wait_ge(rden_ready, cc.n + 1)
                        dve.tensor_tensor(ctxn[:, :, :, :], heads[:, :, :, 0:DK],
                                          rden[:, :, :].rearrange("p t (h o) -> p t h o", o=1)
                                          .broadcast_to([P, NT, H, DK]), ALU.mult).then_inc(ctxn_ready, 1)
                    if s == LN1_OUT and static and i.n == 0:
                        key_rows(0)
                    if s == MISC["wo"] and cc.live():
                        dve.wait_ge(wo_ps, cc.n + 1)
                        dve.wait_ge(xbo_ready, cc.n + 1)
                        dve.tensor_tensor(x_batch(cc), misc[:, 0:S].rearrange("p (t d) -> p t d", t=NT),
                                          x_batch(cc), ALU.add).then_inc(x2_ready, 1)
                        wait_alone(dve, x2_ready, cc.n + 1)
                        statistics(cc, 1, x_tile(cc))
                    if s == MISC["router"] and cc.live():
                        rank(cc)
                    if s == MISC["router"] + 1 and cc.live():
                        combine_weights(cc)
                    if s == MISC["v"] and m.live():
                        dve.wait_ge(v_ps, m.n + 1)
                        if static and m.n == 0:
                            dve.wait_ge(v_cols_ready, 1)
                        for j in range(2):
                            cols = slice(16 * j, 16 * j + DK)
                            ins = dve.tensor_tensor(
                                v_pad[:, m.par, :, :, :].rearrange("p t (k j) e -> p t k j e", j=2)[:, :, :, j, cols],
                                misc[:, 0:S].rearrange("p (t k j d) -> p t k j d", t=NT, j=2, d=DK)[:, :, :, j, :],
                                bv_b[:, :, :].rearrange("p o (k j d) -> p o k j d", j=2, d=DK)[:, :, :, j, :]
                                .broadcast_to([P, NT, H // 2, DK]), ALU.add)
                        ins.then_inc(v_ready, 1)
                if dd.live():
                    dve.wait_ge(out_ps, dd.n + 1)
                    dve.tensor_tensor(x_batch(dd), y_bank[:, 0:S].rearrange("p (t d) -> p t d", t=NT),
                                      x_batch(dd), ALU.add).then_inc(out_ready, 1)
                if static and i.n == 0:
                    key_rows(1)
                    dve.memset(v_pad[:, :, :, :, :], 0.0).then_inc(v_zero, 1)
                    dve.wait_ge(v_zero, 1)
                    ones = v_pad[:, :, :, :, :].rearrange("p b t (k j) e -> p (b t k) j e", j=2)
                    for j in range(2):
                        ins = dve.memset(ones[:, :, j, 16 * j + DK:16 * j + DK + 1], 1.0)
                    ins.then_inc(v_cols_ready, 1)
                if static and i.n == SETUP_STEP:
                    dve.wait_ge(w2_loaded, 16 * LOADS_W2)
                    dve.tensor_scalar(b1_neg[:, :], b1_in[:, :], -1.0, None, ALU.mult).then_inc(b1_neg_ready, 1)
                if static and i.n == SETUP_STEP:
                    dve.wait_ge(setup_bias2, 1)
                    dve.tensor_tensor(bias2[:, :], y_bank[0:E, 0:D], b2_in[:, :], ALU.add).then_inc(bias2_ready, 1)

            steps(dve, one_step)

        @block.tensor
        def _(pe):
            taken = {"shift1": lambda b: (shift_ready[1], b.n + 1), "heads": lambda b: (ctxn_ready, b.n + 1),
                     "ctxT": lambda b: (ctxT_ready, b.n + 1), "wo": lambda b: (x2_ready, b.n + 1),
                     "inT": lambda b: (inT_ready, b.n + 1), "qk": lambda b: (qk_whole_ready, 2 * b.n + 2),
                     "x2T": lambda b: (x2T_copy, 2 * b.n + 2), "router": lambda b: (logits_ready, b.n + 1),
                     "v": lambda b: (v_ready, b.n + 1), "shift0": lambda b: (shift_ready[0], b.n + 1),
                     "cwT": lambda b: (cwT_ready, b.n + 1)}
            last_use = [None]

            def bank_taken():
                if last_use[0]:
                    name, b = last_use[0]
                    pe.wait_ge(*(taken[name](b) if name in taken else b))

            def transpose(dst, src):
                return pe.transpose(dst, src, ident[0:src.shape[0], 0:src.shape[0]])

            def misc_use(name, b):
                bank_taken()
                last_use[0] = (name, b)
                if name in ("shift0", "shift1"):
                    g = int(name[-1])
                    pe.wait_ge(parts_ready[g], b.n + 1)
                    for t in range(NT):
                        last = transpose(misc[0:2 * HG, t * P:(t + 1) * P],
                                         negm_parts[:, g, t, :, :].rearrange("p r h -> p (r h)").bitcast(F32))
                    last.then_inc(shift_ps[g], 1)
                elif name == "heads":
                    pe.wait_ge(o_taken, b.n + 1)
                    for t in range(NT):
                        for g in range(2):
                            c = (t * 2 + g) * P
                            last = transpose(misc[:, c:c + P], oT[:, g, t * P:(t + 1) * P])
                    last.then_inc(heads_ps, 1)
                elif name == "ctxT":
                    pe.wait_ge(ctxn_ready, b.n + 1)
                    for t in range(NT):
                        last = transpose(misc[:, t * P:(t + 1) * P], ctxn[:, t, :, :].rearrange("p h d -> p (h d)"))
                    last.then_inc(ctxT_ps, 1)
                elif name == "wo":
                    pe.wait_ge(ctxT_ready, b.n + 1)
                    pe.wait_ge(wtail_loaded, 16 * LOADS_TAIL)
                    for t in range(NT):
                        last = pe.matmul(misc[:, t * P:(t + 1) * P], ctxT[:, t * P:(t + 1) * P], wo[:, :],
                                         start=True, stop=True)
                    last.then_inc(wo_ps, 1)
                elif name == "inT":
                    pe.wait_ge(xn_ready, NT * b.n + NT)
                    pe.wait_ge(c_loaded, 16 * b.n + 16)
                    for w, src in enumerate((xn, c_cur)):
                        for t in range(NT):
                            c = w * S + t * P
                            last = transpose(misc[:, c:c + P], src[:, b.par, t, :])
                    last.then_inc(inT_ps, 1)
                elif name == "qk":
                    pe.wait_ge(inT_ready, b.n + 1)
                    pe.wait_ge(wqk_loaded, 16 * LOADS_QK)
                    for n, w in enumerate((wq, wk)):
                        last = pe.matmul(misc[:, n * S:(n + 1) * S], w[:, :], inT[:, b.par, n, :],
                                         start=True, stop=True)
                    last.then_inc(qk_ps, 1)
                elif name == "v":
                    pe.wait_ge(wv_loaded, 16 * LOADS_V)
                    for t in range(NT):
                        last = pe.matmul(misc[:, t * P:(t + 1) * P], inT[:, b.par, 1, t * P:(t + 1) * P], wv[:, :],
                                         start=True, stop=True)
                    last.then_inc(v_ps, 1)
                elif name == "x2T":
                    pe.wait_ge(x2n_ready, NT * b.n + NT)
                    for t in range(NT):
                        last = transpose(misc[:, t * P:(t + 1) * P], x2n[:, t, :])
                    last.then_inc(x2T_ps, 1)
                elif name == "router":
                    pe.wait_ge(x2T_copy, 2 * b.n + 1)
                    for t in range(NT):
                        last = pe.matmul(misc[:, t * E:(t + 1) * E], x2T[:, t * P:(t + 1) * P], wr[:, :],
                                         start=True, stop=True)
                    last.then_inc(router_ps, 1)
                elif name == "cwT":
                    pe.wait_ge(cw_ready, b.n + 1)
                    for t in range(NT):
                        last = transpose(misc[0:E, t * P:(t + 1) * P], cw[:, t, :])
                    last.then_inc(cwT_ps, 1)

            def hidden(b, n, m):
                if n == 0:
                    pe.wait_ge(x2T_ready, b.n + 1)
                    pe.wait_ge(w_lo_ready, 2)
                    if m.live():
                        pe.wait_ge(negm_ready, H * m.n)
                elif m.live() and n >= 2:
                    pe.wait_ge(negm_ready, H * m.n + n - 1)
                elif n >= 3:
                    pe.wait_ge(g_ready, TILES * b.n + n - 2)
                z = hidden_bank(n, m)
                for k, (w, xT) in enumerate(((w1_hi, x2T_hi), (w1_hi, x2T_lo), (w1_lo, x2T_hi))):
                    last = pe.matmul(z, w[:, n, :], xT[:, b.par, :], start=k == 0, stop=k == 2)
                last.then_inc(z_ready, 1)

            def down(b, n):
                pe.wait_ge(g_lo_ready, TILES * b.n + n + 1)
                if n == 0:
                    pe.wait_ge(out_ready, b.n + 1)
                    pe.wait_ge(bias2_ready, 1)
                for k, (w, g) in enumerate(((w2_lo, g_hi), (w2_hi, g_hi), (w2_hi, g_lo))):
                    last = pe.matmul(y_bank[:, 0:S], w[:, n, :], g[:, n % G_BUFS, :],
                                     start=n == 0 and k == 0, stop=n == TILES - 1 and k == 2)
                if n == TILES - 1:
                    last.then_inc(y_ready, 1)

            def values(b, q, key_tiles=range(NT)):
                if key_tiles[0] == 0:
                    pe.wait_ge(p_ready, H * b.n + 4 * q + 4)
                if q == 0 and key_tiles[0] == 0:
                    pe.wait_ge(v_ready, b.n + 1)
                    if not isinstance(b.n, int) or b.n > 0:
                        pe.wait_ge(o_taken, b.n)
                g, j = q // 2, q % 2
                for k in key_tiles:
                    for c in range(4):
                        n = 4 * q + c
                        last = pe.matmul(o_bank[32 * c:32 * c + 32, g, :], v_pad[:, b.par, k, head_of(n), :],
                                         probs[:, n % P_BUFS, k, :], start=j == 0 and k == 0,
                                         stop=j == 1 and k == NT - 1)
                if key_tiles[-1] == NT - 1:
                    last.then_inc(p_used, 1)

            def one_step(i):
                a, m, bb, cc, dd = (i.back(lag) for lag in (LAG_A, LAG_M, LAG_B, LAG_C, LAG_D))
                if not isinstance(i.n, int):
                    last_use[0] = ("shift1", bb)
                for s in range(SLOTS):
                    if bb.live():
                        h = head_of(s)
                        if s % HG == 0:
                            pe.wait_ge(shifts_in[s // HG], 16 * (bb.n + 1))
                        if not isinstance(bb.n, int) or H * bb.n + s >= 2:
                            pe.wait_ge(p_ready, H * bb.n + s - 1)
                        for k in range(NT):
                            last = pe.matmul(s_bank[s % 2][:, k, :], Ks[bb.par][:, h, k * P:(k + 1) * P],
                                             Qs[bb.par][:, h, :], start=True, stop=True)
                        last.then_inc(s_ready, 1)
                    if dd.live():
                        if s >= W2_LAG:
                            down(dd, s - W2_LAG)
                        hidden(dd, s, m)
                        if s == BIAS2_SLOT:
                            pe.wait_ge(cwT_ready, dd.n + 1)
                            pe.matmul(y_bank[:, 0:S], bias2[:, :], cwT[:, dd.par, :], start=False, stop=False)
                    if m.live():
                        if s % HG == 0:
                            pe.wait_ge(stacked[s // HG], 16 * stack_dmas(m.n + 1))
                        if dd.live():
                            if s >= 1:
                                pe.wait_ge(g_ready, TILES * dd.n + s)
                        elif H * m.n + s >= 3:
                            pe.wait_ge(negm_ready, H * m.n + max(s - 2, 0))
                        scores = scores_bank(s, dd)
                        for t in range(NT):
                            last = pe.matmul(scores[:, t, :], Qs[m.par][:, s, t * P:(t + 1) * P],
                                             Ks[m.par][:, s, :], start=True, stop=True)
                        last.then_inc(m_ready, 1)
                    if isinstance(i.n, int) and i.n == SETUP_STEP and s >= BIAS_FROM:
                        if s == BIAS_FROM:
                            pe.wait_ge(b1_cols_ready, 1)
                        per_slot = TILES // (SLOTS - BIAS_FROM)
                        for n in range((s - BIAS_FROM) * per_slot, (s - BIAS_FROM + 1) * per_slot):
                            last = pe.matmul(y_bank[0:E, 0:D], b1_cols[:, n, :], w2_in[:, n, :], start=n == 0,
                                             stop=n == TILES - 1)
                        if n == TILES - 1:
                            last.then_inc(setup_bias2, 1)
                    for name, slot in MISC.items():
                        b = i.back(MISC_LAG[name])
                        if slot == s and b.live():
                            misc_use(name, b)
                    if bb.live() and s in VALUES:
                        q, k = VALUES[s]
                        values(bb, q, range(k, k + 1))
                if dd.live():
                    for n in range(TILES - W2_LAG, TILES - 1):
                        down(dd, n)
                if bb.live():
                    values(bb, 3, range(0, 1))
                if dd.live():
                    down(dd, TILES - 1)
                if m.live():
                    misc_use("shift1", m)
                if bb.live():
                    values(bb, 3, range(1, NT))
                if dd.live():
                    pe.wait_ge(y_taken, dd.n + 1)
                    for t in range(NT):
                        last = transpose(y_bank[:, t * P:(t + 1) * P], yT[:, t * P:(t + 1) * P])
                    last.then_inc(out_ps, 1)

            pe.wait_ge(ident_step, 2)
            steps(pe, one_step)


_INS = ['x', 'ctx_1024', 'L0_xattn_Wq', 'L0_xattn_bq', 'L0_xattn_Wk', 'L0_xattn_bk', 'L0_xattn_Wv', 'L0_xattn_bv',
        'L0_xattn_Wo', 'L0_xattn_bo', 'L0_ffn_Wr', 'L0_ffn_br', 'L0_ffn_W1', 'L0_ffn_b1', 'L0_ffn_W2', 'L0_ffn_b2']


def _laid_out(name, a):
    if name in ('x', 'ctx_1024'):
        return a.reshape(B * NT, P, D).transpose(1, 0, 2)
    if name in ('L0_xattn_Wq', 'L0_xattn_Wk', 'L0_xattn_bq', 'L0_xattn_bk'):
        a = a.reshape(-1, 2, HG, DK).transpose(0, 1, 3, 2).reshape(-1, D)
        return a if len(a) > 1 else a.reshape(D, 1)
    if name in ('L0_xattn_bv', 'L0_xattn_bo', 'L0_ffn_br'):
        return a.reshape(1, -1)
    if name == 'L0_ffn_W1':
        return a.transpose(1, 0, 2).reshape(D, TILES, P)
    if name == 'L0_ffn_W2':
        return a.reshape(TILES, P, D).transpose(1, 0, 2)
    if name == 'L0_ffn_b1':
        return a.reshape(TILES, P).transpose(1, 0)
    return a


def kernel(**inputs):
    import numpy as _np
    import concourse.bacc as _bacc
    from concourse import mybir as _mybir
    from concourse.bass_utils import run_bass_kernel_spmd as _run

    nc = _bacc.Bacc("TRN2", target_bir_lowering=False, num_devices=1)
    arrays, args = {}, []
    for name in _INS:
        a = _np.ascontiguousarray(_laid_out(name, _np.asarray(inputs[name])))
        arrays[f"in_{name}_dram"] = a
        args.append(nc.dram_tensor(f"in_{name}_dram", a.shape, _mybir.dt.from_np(a.dtype), kind="ExternalInput").ap())
    args.append(nc.dram_tensor("out_0_dram", (P, B * NT, D), F32, kind="ExternalOutput").ap())
    xattn_moe(nc, *args)
    r = _run(nc, [arrays], core_ids=[0])
    got = _np.asarray(r.results[0]["out_0_dram"])
    return _np.ascontiguousarray(got.transpose(1, 0, 2)).reshape(B, S, D)
```

```python
import concourse.bass as bass
from concourse import mybir
from contextlib import ExitStack

F32 = mybir.dt.float32
F32R = mybir.dt.float32r
U32 = mybir.dt.uint32
ALU = mybir.AluOpType
ACT = mybir.ActivationFunctionType
AX = mybir.AxisListType

B, S, D = 8, 256, 128
H, DK = 16, 8
E, DF = 8, 256
P = 128
NT = S // P
TILES = E * DF // P
HG = 8
SHIFT_ROW = 4 * DK
EPS = 1e-5
EXP_SCALE = float(DK) ** -0.5
P_BUFS = 8
G_BUFS = 4
W2_LAG = 4
SLOTS = 16
AHEAD = 3

LAG_A, LAG_M, LAG_B, LAG_C, LAG_D = 0, 1, 2, 3, 4
STEPS = B + LAG_D
OPENING = -1 - LAG_D
SLOT_OF = {"heads": 1, "ctxT": 3, "wo": 4, "ln1": 6, "ln2_out": 6, "x2T": 7, "router": 8, "rank": 8,
           "ln1_out": 8, "inT": 9, "psum_e": 9, "qk": 10, "combine": 10, "qk_lo": 11, "cwT": 11,
           "shift0": 13, "cw_back": 13, "v": 15}
FILLING_SLOT_OF = dict(SLOT_OF, ln1=0, ln1_out=3, inT=5, qk=6, qk_lo=7, shift0=9, v=11)
FILLED_SLOT_OF = dict(SLOT_OF, ln1=0, ln1_out=2, inT=5, qk=6, qk_lo=6)
EMPTYING_SLOT_OF = dict(SLOT_OF, psum_e=9, combine=9, cwT=10)
VALUES = {5: (0, 0), 6: (0, 1), 8: (1, 0), 10: (1, 1), 12: (2, 0), 13: (2, 1)}
MISC_LAG = {"shift1": LAG_M, "heads": LAG_C, "ctxT": LAG_C, "wo": LAG_C, "inT": LAG_A, "qk": LAG_A,
            "x2T": LAG_C, "router": LAG_C, "v": LAG_M, "shift0": LAG_M, "cwT": LAG_C}
BIAS2_SLOT = 8
SETUP_STEP, BIAS_FROM = 1, 8
LOADS_QK, LOADS_V, LOADS_W2, LOADS_TAIL = 4, 2, 3, 4
PARTS_DMAS = 8
FIRST_WEIGHTS = slice(0, 2), slice(2, E)
ROUTE_CHAIN = 7


class Batch:

    def __init__(self, t, c):
        self.t, self.c = t, c
        self.n = 2 * t + c
        self.par = c % 2

    def back(self, lag):
        return Batch(self.t, self.c - lag)

    def live(self):
        return not isinstance(self.n, int) or 0 <= self.n < B


def stack_dmas(b):
    return (PARTS_DMAS + 1) * (b.t + b.c // 2) + PARTS_DMAS


def slots_of(i):
    if not isinstance(i.n, int) or i.n == B:
        return SLOT_OF
    return FILLING_SLOT_OF if i.n < LAG_C else FILLED_SLOT_OF if i.n == LAG_C else EMPTYING_SLOT_OF


def stages(i):
    a, *later = (i.back(lag) for lag in (LAG_A, LAG_M, LAG_B, LAG_C, LAG_D))
    if isinstance(i.n, int) and i.n == OPENING:
        a = Batch(0, 1)
    elif isinstance(i.n, int) and i.n == 1:
        a = Batch(0, OPENING)
    return a, *later


def head_of(n):
    g, j, c = n // HG, n // 4 % 2, n % 4
    return g * HG + c * 2 + j


def wait_alone(eng, semaphore, value):
    if not isinstance(value, int):
        value = eng.to_reg(value)
        eng.wait_ge(semaphore, 1)
    eng.wait_ge(semaphore, value)


def steps(eng, one_step):
    first, last = LAG_D, B
    for c in range(first):
        one_step(Batch(0, c))
        if c == 0:
            one_step(Batch(0, OPENING))
    with eng.Fori(first // 2, last // 2) as t:
        one_step(Batch(t, 0))
        one_step(Batch(t, 1))
    for c in range(last, STEPS):
        one_step(Batch(0, c))


def xattn_moe(nc, x, ctx_in, Wq, bq, Wk, bk, Wv, bv, Wo, bo, Wr, br, W1, b1, W2, b2, out):
    es = ExitStack()
    with es:
        def sb(name, shape, dt=F32):
            return es.enter_context(nc.sbuf_tensor(name, shape, dt))

        def ps(name, shape):
            return es.enter_context(nc.psum_tensor(name, shape, F32))

        def sem(name):
            return es.enter_context(nc.semaphore(name))

        x_all = sb("x_all", [P, B * NT, D])
        c_cur = sb("c_cur", [P, 2, NT, D])
        xn = sb("xn", [P, 2, NT, D])
        inT = sb("inT", [P, 2, 2, S])
        q_whole = sb("q_whole", [P, S])
        k_whole = sb("k_whole", [P, S])
        q_hi = sb("q_hi", [P, 2, S], F32R)
        q_lo = sb("q_lo", [P, 2, S], F32R)
        k_hi = sb("k_hi", [P, 2, S], F32R)
        k_lo = sb("k_lo", [P, 2, S], F32R)
        Qs = [sb(f"Qs{n}", [P, H, S], F32R) for n in range(2)]
        Ks = [sb(f"Ks{n}", [P, H, S], F32R) for n in range(2)]
        v_pad = sb("v_pad", [P, 2, NT, H, 32])
        negm = sb("negm", [P, 2, NT, H])
        negm_parts = sb("negm_parts", [P, 2, NT, 2, HG], F32R)
        shift_rows = sb("shift_rows", [2 * HG, 2, S], F32R)
        zero_rows = sb("zero_rows", [2 * HG, S])
        probs = sb("probs", [P, P_BUFS, NT, S])
        oT = sb("oT", [P, 2, S])
        rden = sb("rden", [P, NT, H])
        ctxn = sb("ctxn", [P, NT, H, DK])
        ctxT = sb("ctxT", [P, S])
        stats = sb("stats", [P, 2, NT, 6])
        mv = sb("mv", [P, 2, NT, 2])
        rstd = sb("rstd", [P, 2, NT])
        var_eps = sb("var_eps", [P, 2, NT])
        neg_mean = sb("neg_mean", [P, 2, NT])
        nmr = sb("nmr", [P, 2, NT])
        minus_one = sb("minus_one", [P, NT])
        x2n = sb("x2n", [P, NT, D])
        x2T = sb("x2T", [P, S])
        x2T_hi = sb("x2T_hi", [P, 2, S], F32R)
        x2T_lo = sb("x2T_lo", [P, 2, S], F32R)
        logits = sb("logits", [P, NT, E])
        top = sb("top", [P, NT, 8])
        top_i = sb("top_i", [P, NT, 8], U32)
        top_f = sb("top_f", [P, NT, 8])
        shifted = sb("shifted", [P, NT, E])
        pexp = sb("pexp", [P, NT, E])
        psum_e = sb("psum_e", [P, NT])
        rsum_e = sb("rsum_e", [P, NT])
        pick1 = sb("pick1", [P, NT, E])
        pick2 = sb("pick2", [P, NT, E])
        picked = sb("picked", [P, NT, E])
        cw = sb("cw", [P, NT, E])
        cwT = sb("cwT", [E, 2, S])
        cw_b = sb("cw_b", [P, 2, E, S])
        g_t = sb("g_t", [P, G_BUFS, S])
        g_hi = sb("g_hi", [P, G_BUFS, S], F32R)
        g_lo = sb("g_lo", [P, G_BUFS, S], F32R)
        yT = sb("yT", [P, S])
        ident = sb("ident", [P, P])
        empty_turn = sb("empty_turn", [P, 1])
        eps = sb("eps", [P, NT])
        half = sb("half", [P, NT])
        expert_no = sb("expert_no", [P, E])
        wq = sb("wq", [P, D])
        wk = sb("wk", [P, D])
        wv = sb("wv", [P, D])
        wo = sb("wo", [P, D])
        wr = sb("wr", [P, E])
        bq_c = sb("bq_c", [P, 1])
        bk_c = sb("bk_c", [P, 1])
        bv_b = sb("bv_b", [P, 1, D])
        bo_b = sb("bo_b", [P, 1, D])
        br_b = sb("br_b", [P, 1, E])
        w1_hi = sb("w1_hi", [P, TILES, P], F32R)
        w1_lo = sb("w1_lo", [P, TILES, P], F32R)
        w2_hi = sb("w2_hi", [P, TILES, P], F32R)
        w2_lo = sb("w2_lo", [P, TILES, P], F32R)
        w1_in, w2_in = (cw_b[:, n, :, :].rearrange("p e s -> p (e s)").rearrange("p (n d) -> p n d", d=P)
                        for n in range(2))
        b1_in = sb("b1_in", [P, TILES])
        b1_neg = sb("b1_neg", [P, TILES])
        b1_cols = sb("b1_cols", [P, TILES, E])
        b2_in = sb("b2_in", [E, D])
        bias2 = sb("bias2", [E, D])

        s_bank = [ps(f"s_bank{n}", [P, NT, S]) for n in range(2)]
        o_bank = ps("o_bank", [P, 2, S])
        turn_banks = [ps(f"turn_bank{n}", [P, 512]) for n in range(3)]
        y_bank = ps("y_bank", [P, 512])
        misc = ps("misc", [P, 512])

        cw_dram = nc.dram_tensor("cw_scratch", (2, E, S), F32, kind="Internal").ap()

        x0_loaded = sem("x0_loaded")
        x_loaded = sem("x_loaded")
        c0_loaded = sem("c0_loaded")
        c_loaded = sem("c_loaded")
        wqk_loaded = sem("wqk_loaded")
        wv_loaded = sem("wv_loaded")
        wtail_loaded = sem("wtail_loaded")
        w1_loaded = sem("w1_loaded")
        w2_loaded = sem("w2_loaded")
        const_ready = sem("const_ready")
        ident_step = sem("ident_step")
        w_hi_ready = sem("w_hi_ready")
        w_lo_ready = sem("w_lo_ready")
        q_rows_ready = sem("q_rows_ready")
        k_rows_ready = sem("k_rows_ready")
        v_zero = sem("v_zero")
        v_cols_ready = sem("v_cols_ready")
        b1_neg_ready = sem("b1_neg_ready")
        b1_cols_ready = sem("b1_cols_ready")
        bias2_ready = sem("bias2_ready")
        setup_bias2 = sem("setup_bias2")
        stat_ready = [sem("ln1_stat_ready"), sem("ln2_stat_ready")]
        aggr_ready = [sem("ln1_aggr_ready"), sem("ln2_aggr_ready")]
        vareps_ready = [sem("ln1_vareps_ready"), sem("ln2_vareps_ready")]
        rstd_ready = [sem("ln1_rstd_ready"), sem("ln2_rstd_ready")]
        nmr_ready = [sem("ln1_nmr_ready"), sem("ln2_nmr_ready")]
        xn_ready = sem("xn_ready")
        xbo_ready = sem("xbo_ready")
        inT_ps = sem("inT_ps")
        inT_ready = sem("inT_ready")
        qk_ps = sem("qk_ps")
        qk_hi_ready = sem("qk_hi_ready")
        qk_whole_ready = sem("qk_whole_ready")
        qk_lo_ready = sem("qk_lo_ready")
        v_ps = sem("v_ps")
        v_ready = sem("v_ready")
        stacked = [[sem(f"stacked{par}{g}") for g in range(2)] for par in range(2)]
        m_ready = sem("m_ready")
        negm_ready = sem("negm_ready")
        shift_ps = [sem("shift0_ps"), sem("shift1_ps")]
        parts_hi = [sem("parts0_hi"), sem("parts1_hi")]
        parts_ready = [sem("parts0_ready"), sem("parts1_ready")]
        shift_ready = [sem("shift0_ready"), sem("shift1_ready")]
        shifts_in = [sem("shift0_in"), sem("shift1_in")]
        s_ready = sem("s_ready")
        p_ready = sem("p_ready")
        p_used = sem("p_used")
        o_taken = sem("o_taken")
        heads_ps = sem("heads_ps")
        rden_ready = sem("rden_ready")
        ctxn_ready = sem("ctxn_ready")
        ctxT_ps = sem("ctxT_ps")
        ctxT_ready = sem("ctxT_ready")
        wo_ps = sem("wo_ps")
        x2_ready = sem("x2_ready")
        x2n_ready = sem("x2n_ready")
        x2T_ps = sem("x2T_ps")
        x2T_copy = sem("x2T_copy")
        x2T_ready = sem("x2T_ready")
        router_ps = sem("router_ps")
        logits_ready = sem("logits_ready")
        route_step = sem("route_step")
        shifted_ready = sem("shifted_ready")
        pexp_ready = sem("pexp_ready")
        cw_ready = sem("cw_ready")
        cwT_ps = sem("cwT_ps")
        cwT_ready = sem("cwT_ready")
        cw_stored = sem("cw_stored")
        cw_first_ready = sem("cw_first_ready")
        cw_b_ready = sem("cw_b_ready")
        z_ready = sem("z_ready")
        g_ready = sem("g_ready")
        g_hi_ready = sem("g_hi_ready")
        g_lo_ready = sem("g_lo_ready")
        y_ready = sem("y_ready")
        y_taken = sem("y_taken")
        out_ps = sem("out_ps")
        out_ready = sem("out_ready")
        stored = sem("stored")

        block = es.enter_context(nc.Block())

        def hidden_bank(n, heads):
            turn = n + 2 if n < AHEAD else 2 * n - AHEAD if heads else n - 1
            return turn_banks[turn % 3][:, 0:S]

        def scores_bank(h, tiles):
            turn = 2 * h - AHEAD + 1 if h >= AHEAD and tiles else h
            return turn_banks[turn % 3][:, :].rearrange("p (t s) -> p t s", t=NT)

        @block.sync
        def _(sp):
            sp.dma_start(x_all[:, 0:NT, :], x[:, 0:NT, :]).then_inc(x0_loaded, 16)
            sp.dma_start(c_cur[:, 0, :, :], ctx_in[:, 0:NT, :]).then_inc(c0_loaded, 16)
            sp.dma_start(wq[:, :], Wq).then_inc(wqk_loaded, 16)
            sp.dma_start(wk[:, :], Wk).then_inc(wqk_loaded, 16)
            sp.dma_start(bq_c[:, :], bq).then_inc(wqk_loaded, 16)
            sp.dma_start(bk_c[:, :], bk).then_inc(wqk_loaded, 16)
            sp.dma_start(c_cur[:, 1, :, :], ctx_in[:, NT:2 * NT, :]).then_inc(c_loaded, 16)
            sp.dma_start(x_all[:, NT:, :], x[:, NT:, :]).then_inc(x_loaded, 16)
            sp.dma_start(wv[:, :], Wv).then_inc(wv_loaded, 16)
            sp.dma_start(bv_b[:, 0, :], bv.broadcast_to([P, D])).then_inc(wv_loaded, 16)
            sp.dma_start(bo_b[:, 0, :], bo.broadcast_to([P, D])).then_inc(wtail_loaded, 16)
            sp.dma_start(br_b[:, 0, :], br.broadcast_to([P, E])).then_inc(wtail_loaded, 16)
            sp.dma_start(wo[:, :], Wo).then_inc(wtail_loaded, 16)
            sp.dma_start(wr[:, :], Wr).then_inc(wtail_loaded, 16)
            sp.dma_start(w1_in, W1).then_inc(w1_loaded, 16)
            sp.dma_start(w2_in, W2).then_inc(w2_loaded, 16)
            sp.dma_start(b1_in[:, :], b1).then_inc(w2_loaded, 16)
            sp.dma_start(b2_in[:, :], b2).then_inc(w2_loaded, 16)

            def stack(b, g, bb, between=None):
                heads = slice(HG * g, HG * (g + 1))
                rows = slice(64 * g, 64 * g + 64)
                his, los, scores = 2 * b.n + 2, 2 * b.n + 2, H * bb.n + HG * (g + 1)
                if not isinstance(b.n, int):
                    his, los, scores = sp.to_reg(his), sp.to_reg(los), sp.to_reg(scores)
                if bb.live():
                    sp.wait_ge(s_ready, scores)
                if isinstance(b.n, int) and b.n < 2:
                    sp.wait_ge(q_rows_ready, 2 * b.n + g + 1)
                    sp.wait_ge(k_rows_ready, 2 * b.n + g + 1)
                sp.wait_ge(qk_hi_ready, his)
                for r, dst, src in ((0, Qs, q_hi), (0, Ks, k_hi), (1, Qs, q_hi), (2, Ks, k_hi),
                                    (2, Qs, q_lo), (1, Ks, k_lo), (3, Qs, q_lo), (3, Ks, k_lo)):
                    if r == 2 and src is q_lo:
                        if between:
                            shift(*between)
                        sp.wait_ge(qk_lo_ready, los)
                    sp.dma_start(dst[b.par][DK * r:DK * (r + 1), heads, :].bitcast(F32),
                                 src[rows, b.par, :].bitcast(F32)).then_inc(stacked[b.par][g], 16)
                if not isinstance(b.n, int) or b.n >= 2:
                    sp.dma_start(Qs[b.par][SHIFT_ROW:SHIFT_ROW + 2, heads, :].bitcast(F32), zero_rows[:, :])\
                      .then_inc(stacked[b.par][g], 16)

            def shift(b, g):
                heads = slice(HG * g, HG * (g + 1))
                sp.wait_ge(shift_ready[g], b.n + 1)
                sp.dma_start(Qs[b.par][SHIFT_ROW:SHIFT_ROW + 2, heads, :].bitcast(F32),
                             shift_rows[:, g, :].bitcast(F32)).then_inc(shifts_in[g], 16)

            def one_step(i):
                a, m, bb, cc, dd = stages(i)
                if a.live() and not (isinstance(a.n, int) and a.n < 2):
                    sp.dma_start(c_cur[:, a.par, :, :], ctx_in[:, bass.ds(NT * a.n, NT), :])\
                      .then_inc(c_loaded, 16)
                if a.live():
                    stack(a, 0, bb, between=(m, 0) if m.live() else None)
                elif m.live():
                    shift(m, 0)
                if isinstance(i.n, int) and i.n == 1:
                    stack(Batch(0, 1), 1, bb)
                elif a.live() and not (isinstance(i.n, int) and i.n == OPENING):
                    stack(a, 1, bb)
                if m.live():
                    shift(m, 1)
                if dd.live():
                    wait_alone(sp, out_ready, dd.n + 2)
                    sp.dma_start(out[:, bass.ds(NT * dd.n, NT), :],
                                 x_all[:, bass.ds(NT * dd.n, NT), :]).then_inc(stored, 16)

            steps(sp, one_step)
            sp.wait_ge(stored, 16 * B)

        @block.gpsimd
        def _(pool):
            pool.memset(ident[:, :], 0.0).then_inc(ident_step, 1)
            pool.wait_ge(ident_step, 1)
            pool.affine_select(out=ident[:, :], in_=ident[:, :], compare_op=ALU.not_equal, fill=1.0,
                               base=0, pattern=[[-1, P]], channel_multiplier=1).then_inc(ident_step, 1)
            pool.memset(half[:, :], -0.5)
            pool.memset(minus_one[:, :], -1.0)
            pool.memset(eps[:, :], EPS)
            for e in range(E):
                last = pool.memset(expert_no[:, e:e + 1], float(e))
            last.then_inc(const_ready, 1)

            def query_rows(n):
                for g in range(2):
                    pool.memset(Qs[n][:, HG * g:HG * (g + 1), :].bitcast(F32), 0.0).then_inc(q_rows_ready, 1)

            def inverse_root(b, ln):
                pool.wait_ge(aggr_ready[ln], NT * b.n + NT)
                pool.tensor_tensor(neg_mean[:, ln, :], mv[:, ln, :, 0], minus_one[:, :], ALU.mult)
                pool.tensor_tensor(var_eps[:, ln, :], mv[:, ln, :, 1], eps[:, :], ALU.add)\
                    .then_inc(vareps_ready[ln], 1)
                pool.wait_ge(vareps_ready[ln], b.n + 1)
                pool.tensor_tensor(rstd[:, ln, :], var_eps[:, ln, :], half[:, :], ALU.pow)\
                    .then_inc(rstd_ready[ln], 1)
                pool.wait_ge(rstd_ready[ln], b.n + 1)
                pool.tensor_tensor(nmr[:, ln, :], neg_mean[:, ln, :], rstd[:, ln, :], ALU.mult)\
                    .then_inc(nmr_ready[ln], 1)

            def prepare_experts(k):
                if k == 0:
                    pool.wait_ge(w2_loaded, 16 * LOADS_W2)
                    pool.wait_ge(const_ready, 2)
                    for e in range(E):
                        last = pool.tensor_copy(b1_cols[:, 2 * e:2 * e + 2, e], b1_in[:, 2 * e:2 * e + 2])
                    last.then_inc(b1_cols_ready, 1)
                else:
                    pool.wait_ge(setup_bias2, 1)
                w_lo, w_in, w_hi = ((w1_lo, w1_in, w1_hi), (w2_lo, w2_in, w2_hi))[k]
                pool.wait_ge(w_hi_ready, k + 1)
                pool.tensor_tensor(w_lo[:, :, :], w_in, w_hi[:, :, :].bitcast(F32), ALU.subtract)\
                    .then_inc(w_lo_ready, 1)

            def second_part(b, n):
                pool.wait_ge(g_hi_ready, TILES * b.n + n + 1)
                pool.tensor_tensor(g_lo[:, n % G_BUFS, :], g_t[:, n % G_BUFS, :],
                                   g_hi[:, n % G_BUFS, :].bitcast(F32), ALU.subtract).then_inc(g_lo_ready, 1)

            def one_step(i):
                at = slots_of(i)
                a, m, bb, cc, dd = stages(i)
                if isinstance(i.n, int) and i.n == 0:
                    inverse_root(a, 0)
                    query_rows(0)
                for s in range(SLOTS):
                    if dd.live() and s >= AHEAD:
                        second_part(dd, s)
                    if s == at["ln1"] and a.live() and not (isinstance(a.n, int) and a.n == 0):
                        if isinstance(a.n, int) and a.n == 1:
                            pool.wait_ge(xn_ready, NT)
                        inverse_root(a, 0)
                    if s == at["wo"] and cc.live():
                        inverse_root(cc, 1)
                    if s == at["ln1_out"] and isinstance(i.n, int) and i.n == OPENING:
                        query_rows(1)
                        pool.memset(zero_rows[:, :], 0.0)
                        pool.memset(b1_cols[:, :, :], 0.0).then_inc(const_ready, 1)
                    if s == at["qk_lo"] and a.live():
                        pool.wait_ge(qk_hi_ready, 2 * a.n + 2)
                        for whole, hi, lo in ((q_whole, q_hi, q_lo), (k_whole, k_hi, k_lo)):
                            pool.tensor_tensor(lo[:, a.par, :], whole[:, :], hi[:, a.par, :].bitcast(F32),
                                               ALU.subtract).then_inc(qk_lo_ready, 1)
                    if s == at["qk_lo"] and a.live():
                        pool.wait_ge(wtail_loaded, 16 * LOADS_TAIL)
                        pool.wait_ge(xn_ready, NT * a.n + NT)
                        xb = x_all[:, bass.ds(NT * a.n, NT), :]
                        pool.tensor_tensor(xb, xb, bo_b[:, :, :].broadcast_to([P, NT, D]), ALU.add)\
                            .then_inc(xbo_ready, 1)
                    if s == at["qk_lo"] and isinstance(i.n, int) and i.n in (SETUP_STEP, SETUP_STEP + 1):
                        prepare_experts(i.n - SETUP_STEP)
                    if s == at["x2T"] and cc.live():
                        pool.wait_ge(x2T_copy, 2 * cc.n + 2)
                        pool.tensor_tensor(x2T_lo[:, cc.par, :], x2T[:, :], x2T_hi[:, cc.par, :].bitcast(F32),
                                           ALU.subtract).then_inc(x2T_ready, 1)
                if cc.live():
                    for n in range(AHEAD):
                        second_part(cc, n)

            pool.wait_ge(const_ready, 1)
            steps(pool, one_step)

        @block.scalar
        def _(act):
            def normalise(b, ln, dst, done):
                act.wait_ge(nmr_ready[ln], b.n + 1)
                for t in range(NT):
                    act.activation(dst[:, t, :], x_all[:, bass.ds(NT * b.n + t, 1), :], ACT.Identity,
                                   bias=nmr[:, ln, t:t + 1], scale=rstd[:, ln, t:t + 1]).then_inc(done, 1)

            def first_part(b, n):
                act.wait_ge(g_ready, TILES * b.n + n + 1)
                act.activation(g_hi[:, n % G_BUFS, :], g_t[:, n % G_BUFS, :], ACT.Copy).then_inc(g_hi_ready, 1)

            def take_shift(b, g):
                act.wait_ge(shift_ps[g], b.n + 1)
                act.activation(shift_rows[:, g, :], misc[0:2 * HG, 0:S], ACT.Copy).then_inc(shift_ready[g], 1)

            def one_step(i):
                at = slots_of(i)
                a, m, bb, cc, dd = stages(i)
                if isinstance(i.n, int) and i.n == SETUP_STEP:
                    act.wait_ge(w1_loaded, 16)
                    act.activation(w1_hi[:, :, :], w1_in, ACT.Copy).then_inc(w_hi_ready, 1)
                    act.wait_ge(w2_loaded, 16 * LOADS_W2)
                    act.activation(w2_hi[:, :, :], w2_in, ACT.Copy).then_inc(w_hi_ready, 1)
                for s in range(SLOTS):
                    if bb.live():
                        n = H * bb.n + s
                        act.wait_ge(s_ready, n + 1)
                        if s % 4 == 0 and (not isinstance(bb.n, int) or bb.n > 0 or s >= P_BUFS):
                            act.wait_ge(p_used, 4 * bb.n + s // 4 + 1 - P_BUFS // 4)
                        act.activation(probs[:, s % P_BUFS, :, :], s_bank[s % 2][:, :, :], ACT.Exp,
                                       scale=EXP_SCALE).then_inc(p_ready, 1)
                    if dd.live() and s >= AHEAD:
                        first_part(dd, s)
                    if s == at["ln1_out"] and a.live():
                        normalise(a, 0, xn[:, a.par, :, :], xn_ready)
                    if s == at["ln2_out"] and cc.live():
                        normalise(cc, 1, x2n, x2n_ready)
                    if s == at["ctxT"] and cc.live():
                        act.wait_ge(ctxT_ps, cc.n + 1)
                        act.activation(ctxT[:, :], misc[:, 0:S], ACT.Copy).then_inc(ctxT_ready, 1)
                    if s == at["inT"] and a.live():
                        act.wait_ge(inT_ps, a.n + 1)
                        act.activation(inT[:, a.par, :, :], misc[:, :].rearrange("p (w t) -> p w t", w=2),
                                       ACT.Copy).then_inc(inT_ready, 1)
                    if s == at["qk"] and a.live():
                        act.wait_ge(qk_ps, a.n + 1)
                        act.activation(q_whole[:, :], misc[:, 0:S], ACT.Identity, bias=bq_c[:, :])\
                           .then_inc(qk_whole_ready, 1)
                        act.activation(k_whole[:, :], misc[:, S:2 * S], ACT.Identity, bias=bk_c[:, :])\
                           .then_inc(qk_whole_ready, 1)
                        act.wait_ge(qk_whole_ready, 2 * a.n + 2)
                        act.activation(q_hi[:, a.par, :], q_whole[:, :], ACT.Copy).then_inc(qk_hi_ready, 1)
                        act.activation(k_hi[:, a.par, :], k_whole[:, :], ACT.Copy).then_inc(qk_hi_ready, 1)
                    if s == at["x2T"] and cc.live():
                        act.wait_ge(x2T_ps, cc.n + 1)
                        act.activation(x2T[:, :], misc[:, 0:S], ACT.Copy).then_inc(x2T_copy, 1)
                        act.activation(x2T_hi[:, cc.par, :], misc[:, 0:S], ACT.Copy).then_inc(x2T_copy, 1)
                    if s == at["rank"] and cc.live():
                        act.wait_ge(shifted_ready, cc.n + 1)
                        act.activation(pexp[:, :, :], shifted[:, :, :], ACT.Exp).then_inc(pexp_ready, 1)
                    if s == at["shift0"] and m.live():
                        take_shift(m, 0)
                    if s == at["cwT"] and cc.live():
                        act.wait_ge(cwT_ps, cc.n + 1)
                        act.activation(cwT[:, cc.par, :], misc[0:E, 0:S], ACT.Copy).then_inc(cwT_ready, 1)
                        if not isinstance(cc.n, int) or cc.n >= 2:
                            act.wait_ge(cw_b_ready, 16 * cc.n - 16)
                        act.wait_ge(cwT_ready, cc.n + 1)
                        act.dma_start(cw_dram[cc.par], cwT[:, cc.par, :]).then_inc(cw_stored, 16)
                    if s == at["cwT"] + 2 and cc.live():
                        if isinstance(cc.n, int) and cc.n == 0:
                            act.wait_ge(w_lo_ready, 2)
                        act.wait_ge(cw_stored, 16 * cc.n + 16)
                        for e, done in zip(FIRST_WEIGHTS, (cw_first_ready, cw_b_ready)):
                            act.dma_start(cw_b[:, cc.par, e, :],
                                          cw_dram[cc.par:cc.par + 1, e, :].broadcast_to([P, e.stop - e.start, S]))\
                               .then_inc(done, 16)
                if cc.live():
                    for n in range(AHEAD):
                        first_part(cc, n)
                if dd.live():
                    act.wait_ge(y_ready, dd.n + 1)
                    act.activation(yT[:, :], y_bank[:, 0:S], ACT.Copy).then_inc(y_taken, 1)
                if m.live():
                    take_shift(m, 1)
                if bb.live():
                    act.wait_ge(p_used, 4 * bb.n + 4)
                    act.activation(oT[:, :, :], o_bank[:, :, :], ACT.Copy).then_inc(o_taken, 1)

            steps(act, one_step)

        @block.vector
        def _(dve):
            def key_rows(n):
                for g in range(2):
                    heads = slice(HG * g, HG * (g + 1))
                    dve.memset(Ks[n][:, heads, :].bitcast(F32), 1.0).then_inc(k_rows_ready, 1)

            dve.memset(empty_turn[:, :], 0.0).then_inc(out_ready, 1)

            def statistics(b, ln, src):
                for t in range(NT):
                    last = dve.bn_stats(stats[:, ln, t, :], src(t))
                last.then_inc(stat_ready[ln], 1)
                wait_alone(dve, stat_ready[ln], b.n + 1)
                for t in range(NT):
                    dve.bn_aggr(mv[:, ln, t, :], stats[:, ln, t, :]).then_inc(aggr_ready[ln], 1)

            def split_maxima(b, g):
                whole = negm[:, b.par, :, HG * g:HG * (g + 1)]
                wait_alone(dve, negm_ready, H * b.n + HG * (g + 1))
                dve.tensor_copy(negm_parts[:, g, :, 0, :], whole).then_inc(parts_hi[g], 1)
                dve.wait_ge(parts_hi[g], b.n + 1)
                dve.tensor_tensor(negm_parts[:, g, :, 1, :], whole, negm_parts[:, g, :, 0, :].bitcast(F32),
                                  ALU.subtract).then_inc(parts_ready[g], 1)

            def gate(b, n, m):
                dve.wait_ge(z_ready, TILES * b.n + n + 1)
                if n in (0, FIRST_WEIGHTS[0].stop * (TILES // E)):
                    dve.wait_ge(cw_first_ready if n == 0 else cw_b_ready, 16 * b.n + 16)
                dve.scalar_tensor_tensor(g_t[:, n % G_BUFS, :], hidden_bank(n, m.live()), b1_neg[:, n:n + 1],
                                         cw_b[:, b.par, n // 2, :], op0=ALU.max, op1=ALU.mult)\
                   .then_inc(g_ready, 1)

            def x_tile(b):
                return lambda t: x_all[:, bass.ds(NT * b.n + t, 1), :]

            def x_batch(b):
                return x_all[:, bass.ds(NT * b.n, NT), :]

            def routed(b, links):
                dve.wait_ge(route_step, ROUTE_CHAIN * b.n + links)

            def top_two(b):
                dve.wait_ge(router_ps, b.n + 1)
                dve.tensor_tensor(logits[:, :, :], misc[:, 0:NT * E].rearrange("p (t e) -> p t e", t=NT),
                                  br_b[:, :, :].broadcast_to([P, NT, E]), ALU.add).then_inc(logits_ready, 1)
                wait_alone(dve, logits_ready, b.n + 1)
                dve.max(out=top[:, 0, :], in_=logits[:, 0, :])
                dve.max(out=top[:, 1, :], in_=logits[:, 1, :]).then_inc(route_step, 1)

            def rank(b):
                routed(b, 1)
                dve.tensor_tensor(shifted[:, :, :], logits[:, :, :], top[:, :, 0:1].broadcast_to([P, NT, E]),
                                  ALU.subtract).then_inc(shifted_ready, 1)
                dve.max_index(top_i[:, 0, :], top[:, 0, :], logits[:, 0, :])
                dve.max_index(top_i[:, 1, :], top[:, 1, :], logits[:, 1, :]).then_inc(route_step, 1)

            def sum_of_experts(b):
                routed(b, 2)
                dve.tensor_copy(top_f[:, :, :], top_i[:, :, :]).then_inc(route_step, 1)
                dve.wait_ge(pexp_ready, b.n + 1)
                dve.tensor_reduce(psum_e[:, :], pexp[:, :, :], AX.X, ALU.add).then_inc(route_step, 1)

            def combine_weights(b):
                routed(b, 4)
                dve.reciprocal(rsum_e[:, :], psum_e[:, :]).then_inc(route_step, 1)
                for t in range(NT):
                    for pick, k in ((pick1, 0), (pick2, 1)):
                        last = dve.scalar_tensor_tensor(pick[:, t, :], expert_no[:, :], top_f[:, t, k:k + 1],
                                                        pexp[:, t, :], op0=ALU.is_equal, op1=ALU.mult)
                last.then_inc(route_step, 1)
                routed(b, 6)
                dve.tensor_tensor(picked[:, :, :], pick1[:, :, :], pick2[:, :, :], ALU.add).then_inc(route_step, 1)
                routed(b, 7)
                dve.tensor_tensor(cw[:, :, :], picked[:, :, :],
                                  rsum_e[:, :].rearrange("p (t o) -> p t o", o=1).broadcast_to([P, NT, E]),
                                  ALU.mult).then_inc(cw_ready, 1)

            def one_step(i):
                at = slots_of(i)
                a, m, bb, cc, dd = stages(i)
                static = isinstance(i.n, int)
                for s in range(SLOTS):
                    if dd.live() and s >= AHEAD:
                        gate(dd, s, m)
                    if m.live():
                        dve.wait_ge(m_ready, H * m.n + s + 1)
                        dve.tensor_reduce(negm[:, m.par, :, s], scores_bank(s, dd.live()), AX.X, ALU.max, negate=True)\
                           .then_inc(negm_ready, 1)
                        if s % HG == HG - 1:
                            split_maxima(m, s // HG)
                    if s == at["ln1"] and a.live():
                        if static and a.n == 0:
                            dve.wait_ge(x0_loaded, 16)
                        else:
                            dve.wait_ge(x_loaded, 16)
                        if static and a.n == 1:
                            dve.wait_ge(nmr_ready[0], 1)
                        statistics(a, 0, x_tile(a))
                    if s == at["heads"] and cc.live():
                        dve.wait_ge(heads_ps, cc.n + 1)
                        heads = misc[:, :].rearrange("p (t h e) -> p t h e", t=NT, h=H)
                        dve.reciprocal(rden[:, :, :], heads[:, :, :, DK]).then_inc(rden_ready, 1)
                        dve.wait_ge(rden_ready, cc.n + 1)
                        dve.tensor_tensor(ctxn[:, :, :, :], heads[:, :, :, 0:DK],
                                          rden[:, :, :].rearrange("p t (h o) -> p t h o", o=1)
                                          .broadcast_to([P, NT, H, DK]), ALU.mult).then_inc(ctxn_ready, 1)
                    if s == at["ln1_out"] and static and i.n == 0:
                        key_rows(0)
                    if s == at["wo"] and cc.live():
                        dve.wait_ge(wo_ps, cc.n + 1)
                        dve.wait_ge(xbo_ready, cc.n + 1)
                        dve.tensor_tensor(x_batch(cc), misc[:, 0:S].rearrange("p (t d) -> p t d", t=NT),
                                          x_batch(cc), ALU.add).then_inc(x2_ready, 1)
                        wait_alone(dve, x2_ready, cc.n + 1)
                        statistics(cc, 1, x_tile(cc))
                    if s == at["router"] and cc.live():
                        top_two(cc)
                    if s == at["rank"] and cc.live():
                        rank(cc)
                    if s == at["psum_e"] and cc.live():
                        sum_of_experts(cc)
                    if s == at["combine"] and cc.live():
                        combine_weights(cc)
                    if s == at["v"] and m.live():
                        dve.wait_ge(v_ps, m.n + 1)
                        if static and m.n == 0:
                            dve.wait_ge(v_cols_ready, 1)
                        for j in range(2):
                            cols = slice(16 * j, 16 * j + DK)
                            ins = dve.tensor_tensor(
                                v_pad[:, m.par, :, :, :].rearrange("p t (k j) e -> p t k j e", j=2)[:, :, :, j, cols],
                                misc[:, 0:S].rearrange("p (t k j d) -> p t k j d", t=NT, j=2, d=DK)[:, :, :, j, :],
                                bv_b[:, :, :].rearrange("p o (k j d) -> p o k j d", j=2, d=DK)[:, :, :, j, :]
                                .broadcast_to([P, NT, H // 2, DK]), ALU.add)
                        ins.then_inc(v_ready, 1)
                if cc.live():
                    for n in range(AHEAD):
                        gate(cc, n, m)
                if dd.live():
                    dve.wait_ge(out_ps, dd.n + 1)
                    dve.tensor_tensor(x_batch(dd), y_bank[:, 0:S].rearrange("p (t d) -> p t d", t=NT),
                                      x_batch(dd), ALU.add).then_inc(out_ready, 1)
                if static and i.n == OPENING:
                    key_rows(1)
                    dve.memset(v_pad[:, :, :, :, :], 0.0).then_inc(v_zero, 1)
                    dve.wait_ge(v_zero, 1)
                    ones = v_pad[:, :, :, :, :].rearrange("p b t (k j) e -> p (b t k) j e", j=2)
                    for j in range(2):
                        ins = dve.memset(ones[:, :, j, 16 * j + DK:16 * j + DK + 1], 1.0)
                    ins.then_inc(v_cols_ready, 1)
                if static and i.n == SETUP_STEP:
                    dve.wait_ge(w2_loaded, 16 * LOADS_W2)
                    dve.tensor_scalar(b1_neg[:, :], b1_in[:, :], -1.0, None, ALU.mult).then_inc(b1_neg_ready, 1)
                if static and i.n == SETUP_STEP:
                    dve.wait_ge(setup_bias2, 1)
                    dve.tensor_tensor(bias2[:, :], y_bank[0:E, 0:D], b2_in[:, :], ALU.add).then_inc(bias2_ready, 1)

            steps(dve, one_step)

        @block.tensor
        def _(pe):
            taken = {"shift1": lambda b: (shift_ready[1], b.n + 1), "heads": lambda b: (ctxn_ready, b.n + 1),
                     "ctxT": lambda b: (ctxT_ready, b.n + 1), "wo": lambda b: (x2_ready, b.n + 1),
                     "inT": lambda b: (inT_ready, b.n + 1), "qk": lambda b: (qk_whole_ready, 2 * b.n + 2),
                     "x2T": lambda b: (x2T_copy, 2 * b.n + 2), "router": lambda b: (logits_ready, b.n + 1),
                     "v": lambda b: (v_ready, b.n + 1), "shift0": lambda b: (shift_ready[0], b.n + 1),
                     "cwT": lambda b: (cwT_ready, b.n + 1)}
            last_use = [None]

            def bank_taken():
                if last_use[0]:
                    name, b = last_use[0]
                    pe.wait_ge(*(taken[name](b) if name in taken else b))

            def transpose(dst, src):
                return pe.transpose(dst, src, ident[0:src.shape[0], 0:src.shape[0]])

            def misc_use(name, b):
                bank_taken()
                last_use[0] = (name, b)
                if name in ("shift0", "shift1"):
                    g = int(name[-1])
                    pe.wait_ge(parts_ready[g], b.n + 1)
                    for t in range(NT):
                        last = transpose(misc[0:2 * HG, t * P:(t + 1) * P],
                                         negm_parts[:, g, t, :, :].rearrange("p r h -> p (r h)").bitcast(F32))
                    last.then_inc(shift_ps[g], 1)
                elif name == "heads":
                    pe.wait_ge(o_taken, b.n + 1)
                    for t in range(NT):
                        for g in range(2):
                            c = (t * 2 + g) * P
                            last = transpose(misc[:, c:c + P], oT[:, g, t * P:(t + 1) * P])
                    last.then_inc(heads_ps, 1)
                elif name == "ctxT":
                    pe.wait_ge(ctxn_ready, b.n + 1)
                    for t in range(NT):
                        last = transpose(misc[:, t * P:(t + 1) * P], ctxn[:, t, :, :].rearrange("p h d -> p (h d)"))
                    last.then_inc(ctxT_ps, 1)
                elif name == "wo":
                    pe.wait_ge(ctxT_ready, b.n + 1)
                    pe.wait_ge(wtail_loaded, 16 * LOADS_TAIL)
                    for t in range(NT):
                        last = pe.matmul(misc[:, t * P:(t + 1) * P], ctxT[:, t * P:(t + 1) * P], wo[:, :],
                                         start=True, stop=True)
                    last.then_inc(wo_ps, 1)
                elif name == "inT":
                    pe.wait_ge(xn_ready, NT * b.n + NT)
                    if isinstance(b.n, int) and b.n == 0:
                        pe.wait_ge(c0_loaded, 16)
                    else:
                        pe.wait_ge(c_loaded, 16 * b.n)
                    for w, src in enumerate((xn, c_cur)):
                        for t in range(NT):
                            c = w * S + t * P
                            last = transpose(misc[:, c:c + P], src[:, b.par, t, :])
                    last.then_inc(inT_ps, 1)
                elif name == "qk":
                    pe.wait_ge(inT_ready, b.n + 1)
                    pe.wait_ge(wqk_loaded, 16 * LOADS_QK)
                    for n, w in enumerate((wq, wk)):
                        last = pe.matmul(misc[:, n * S:(n + 1) * S], w[:, :], inT[:, b.par, n, :],
                                         start=True, stop=True)
                    last.then_inc(qk_ps, 1)
                elif name == "v":
                    pe.wait_ge(wv_loaded, 16 * LOADS_V)
                    for t in range(NT):
                        last = pe.matmul(misc[:, t * P:(t + 1) * P], inT[:, b.par, 1, t * P:(t + 1) * P], wv[:, :],
                                         start=True, stop=True)
                    last.then_inc(v_ps, 1)
                elif name == "x2T":
                    pe.wait_ge(x2n_ready, NT * b.n + NT)
                    for t in range(NT):
                        last = transpose(misc[:, t * P:(t + 1) * P], x2n[:, t, :])
                    last.then_inc(x2T_ps, 1)
                elif name == "router":
                    pe.wait_ge(x2T_copy, 2 * b.n + 1)
                    for t in range(NT):
                        last = pe.matmul(misc[:, t * E:(t + 1) * E], x2T[:, t * P:(t + 1) * P], wr[:, :],
                                         start=True, stop=True)
                    last.then_inc(router_ps, 1)
                elif name == "cwT":
                    pe.wait_ge(cw_ready, b.n + 1)
                    for t in range(NT):
                        last = transpose(misc[0:E, t * P:(t + 1) * P], cw[:, t, :])
                    last.then_inc(cwT_ps, 1)

            def hidden(b, n, m, d):
                if n == 0:
                    pe.wait_ge(x2T_ready, b.n + 1)
                    pe.wait_ge(w_lo_ready, 2)
                if n < AHEAD:
                    if m.live():
                        pe.wait_ge(negm_ready, H * m.n + min(H - 1 + n, H))
                    if d.live() and n == (1 if m.live() else 0):
                        pe.wait_ge(g_ready, TILES * d.n + TILES)
                elif m.live():
                    pe.wait_ge(negm_ready, H * m.n + n - 1)
                else:
                    pe.wait_ge(g_ready, TILES * b.n + n - 2)
                z = hidden_bank(n, m.live())
                for k, (w, xT) in enumerate(((w1_hi, x2T_hi), (w1_hi, x2T_lo), (w1_lo, x2T_hi))):
                    last = pe.matmul(z, w[:, n, :], xT[:, b.par, :], start=k == 0, stop=k == 2)
                last.then_inc(z_ready, 1)

            def down(b, n):
                pe.wait_ge(g_lo_ready, TILES * b.n + n + 1)
                if n == 0:
                    pe.wait_ge(out_ready, b.n + 1)
                    pe.wait_ge(bias2_ready, 1)
                for k, (w, g) in enumerate(((w2_lo, g_hi), (w2_hi, g_hi), (w2_hi, g_lo))):
                    last = pe.matmul(y_bank[:, 0:S], w[:, n, :], g[:, n % G_BUFS, :],
                                     start=n == 0 and k == 0, stop=n == TILES - 1 and k == 2)
                if n == TILES - 1:
                    last.then_inc(y_ready, 1)

            def values(b, q, key_tiles=range(NT)):
                if key_tiles[0] == 0:
                    pe.wait_ge(p_ready, H * b.n + 4 * q + 4)
                if q == 0 and key_tiles[0] == 0:
                    pe.wait_ge(v_ready, b.n + 1)
                    if not isinstance(b.n, int) or b.n > 0:
                        pe.wait_ge(o_taken, b.n)
                g, j = q // 2, q % 2
                for k in key_tiles:
                    for c in range(4):
                        n = 4 * q + c
                        last = pe.matmul(o_bank[32 * c:32 * c + 32, g, :], v_pad[:, b.par, k, head_of(n), :],
                                         probs[:, n % P_BUFS, k, :], start=j == 0 and k == 0,
                                         stop=j == 1 and k == NT - 1)
                if key_tiles[-1] == NT - 1:
                    last.then_inc(p_used, 1)

            def one_step(i):
                at = slots_of(i)
                a, m, bb, cc, dd = stages(i)
                if not isinstance(i.n, int):
                    last_use[0] = ("shift1", bb)
                for s in range(SLOTS):
                    if bb.live():
                        h = head_of(s)
                        if s % HG == 0:
                            pe.wait_ge(shifts_in[s // HG], 16 * (bb.n + 1))
                        if not isinstance(bb.n, int) or H * bb.n + s >= 2:
                            pe.wait_ge(p_ready, H * bb.n + s - 1)
                        for k in range(NT):
                            last = pe.matmul(s_bank[s % 2][:, k, :], Ks[bb.par][:, h, k * P:(k + 1) * P],
                                             Qs[bb.par][:, h, :], start=True, stop=True)
                        last.then_inc(s_ready, 1)
                    if dd.live():
                        if s >= W2_LAG:
                            down(dd, s - W2_LAG)
                        if s >= AHEAD:
                            hidden(dd, s, m, dd)
                        if s == BIAS2_SLOT:
                            pe.wait_ge(cwT_ready, dd.n + 1)
                            pe.matmul(y_bank[:, 0:S], bias2[:, :], cwT[:, dd.par, :], start=False, stop=False)
                    if m.live():
                        if s % HG == 0:
                            pe.wait_ge(stacked[m.par][s // HG], 16 * stack_dmas(m))
                        if dd.live():
                            if s != 2:
                                pe.wait_ge(g_ready, TILES * dd.n + (min(s + 2, AHEAD) if s < AHEAD + 1 else s))
                            if s == AHEAD:
                                pe.wait_ge(negm_ready, H * m.n + AHEAD - 1)
                        elif H * m.n + s >= 3:
                            pe.wait_ge(negm_ready, H * m.n + max(s - 2, 0))
                        scores = scores_bank(s, dd.live())
                        for t in range(NT):
                            last = pe.matmul(scores[:, t, :], Qs[m.par][:, s, t * P:(t + 1) * P],
                                             Ks[m.par][:, s, :], start=True, stop=True)
                        last.then_inc(m_ready, 1)
                    if isinstance(i.n, int) and i.n == SETUP_STEP and s >= BIAS_FROM:
                        if s == BIAS_FROM:
                            pe.wait_ge(b1_cols_ready, 1)
                        per_slot = TILES // (SLOTS - BIAS_FROM)
                        for n in range((s - BIAS_FROM) * per_slot, (s - BIAS_FROM + 1) * per_slot):
                            last = pe.matmul(y_bank[0:E, 0:D], b1_cols[:, n, :], w2_in[:, n, :], start=n == 0,
                                             stop=n == TILES - 1)
                        if n == TILES - 1:
                            last.then_inc(setup_bias2, 1)
                    for name, lag in MISC_LAG.items():
                        b = (a, m, bb, cc, dd)[lag]
                        if at.get(name) == s and b.live():
                            misc_use(name, b)
                    if bb.live() and s in VALUES:
                        q, k = VALUES[s]
                        values(bb, q, range(k, k + 1))
                for n in range(AHEAD):
                    if dd.live():
                        down(dd, TILES - W2_LAG + n)
                    if n == AHEAD - 1 and bb.live():
                        values(bb, 3, range(0, 1))
                    if cc.live():
                        hidden(cc, n, m, dd)
                if dd.live():
                    down(dd, TILES - 1)
                if m.live():
                    misc_use("shift1", m)
                if bb.live():
                    values(bb, 3, range(1, NT))
                if dd.live():
                    pe.wait_ge(y_taken, dd.n + 1)
                    for t in range(NT):
                        last = transpose(y_bank[:, t * P:(t + 1) * P], yT[:, t * P:(t + 1) * P])
                    last.then_inc(out_ps, 1)

            pe.wait_ge(ident_step, 2)
            steps(pe, one_step)


_INS = ['x', 'ctx_1024', 'L0_xattn_Wq', 'L0_xattn_bq', 'L0_xattn_Wk', 'L0_xattn_bk', 'L0_xattn_Wv', 'L0_xattn_bv',
        'L0_xattn_Wo', 'L0_xattn_bo', 'L0_ffn_Wr', 'L0_ffn_br', 'L0_ffn_W1', 'L0_ffn_b1', 'L0_ffn_W2', 'L0_ffn_b2']


def _laid_out(name, a):
    if name in ('x', 'ctx_1024'):
        return a.reshape(B * NT, P, D).transpose(1, 0, 2)
    if name in ('L0_xattn_Wq', 'L0_xattn_Wk', 'L0_xattn_bq', 'L0_xattn_bk'):
        a = a.reshape(-1, 2, HG, DK).transpose(0, 1, 3, 2).reshape(-1, D)
        return a if len(a) > 1 else a.reshape(D, 1)
    if name in ('L0_xattn_bv', 'L0_xattn_bo', 'L0_ffn_br'):
        return a.reshape(1, -1)
    if name == 'L0_ffn_W1':
        return a.transpose(1, 0, 2).reshape(D, TILES, P)
    if name == 'L0_ffn_W2':
        return a.reshape(TILES, P, D).transpose(1, 0, 2)
    if name == 'L0_ffn_b1':
        return a.reshape(TILES, P).transpose(1, 0)
    return a


def kernel(**inputs):
    import numpy as _np
    import concourse.bacc as _bacc
    from concourse import mybir as _mybir
    from concourse.bass_utils import run_bass_kernel_spmd as _run

    nc = _bacc.Bacc("TRN2", target_bir_lowering=False, num_devices=1)
    arrays, args = {}, []
    for name in _INS:
        a = _np.ascontiguousarray(_laid_out(name, _np.asarray(inputs[name])))
        arrays[f"in_{name}_dram"] = a
        args.append(nc.dram_tensor(f"in_{name}_dram", a.shape, _mybir.dt.from_np(a.dtype), kind="ExternalInput").ap())
    args.append(nc.dram_tensor("out_0_dram", (P, B * NT, D), F32, kind="ExternalOutput").ap())
    xattn_moe(nc, *args)
    r = _run(nc, [arrays], core_ids=[0])
    got = _np.asarray(r.results[0]["out_0_dram"])
    return _np.ascontiguousarray(got.transpose(1, 0, 2)).reshape(B, S, D)
```
